# Optimizing a Trainium2 kernel written in Bass

```python
import numpy as np
import jax
import jax.numpy as jnp

def _softmax(x, axis=-1):
    return jax.nn.softmax(x, axis=axis)

def _gelu(x):
    return jax.nn.gelu(x, approximate=True)

def _silu(x):
    return jax.nn.silu(x)

def _sigmoid(x):
    return jax.nn.sigmoid(x)

def _layernorm(x, axis=-1, eps=1e-05):
    m = jnp.mean(x, axis=axis, keepdims=True)
    v = jnp.var(x, axis=axis, keepdims=True)
    return (x - m) / jnp.sqrt(v + eps)

def _scatter_add(tgt, idx, src, axis=0):
    return tgt.at[idx].add(src)

def _segment_sum(src, seg, n):
    return jax.ops.segment_sum(src, seg, n)
kernel_name = 'mk_adaln_attn_ffn_d1_seqx_r4_74dc9a'

def setup_inputs(seed: int=0):
    np.random.seed(seed)
    _w = jnp.asarray

    def _rec_inputs():
        import jax
        import jax.numpy as jnp
        _rk = jax.random.key(seed)
        x = -0.0003929 + 0.9999 * jax.random.normal(jax.random.fold_in(_rk, 1), (64, 64, 256), jnp.float32)
        _lenS = 64 - jax.random.randint(jax.random.fold_in(_rk, 7), (64,), 0, max(1, 64 // 4) + 1, jnp.int32)
        _lenS2 = 64 - jax.random.randint(jax.random.fold_in(_rk, 8), (64,), 0, max(1, 64 // 4) + 1, jnp.int32)
        itok_B_0_15 = jax.random.randint(jax.random.fold_in(_rk, 11), (64,), 0, 16, jnp.int32)
        itok_B_0_3 = jax.random.randint(jax.random.fold_in(_rk, 12), (64,), 0, 4, jnp.int32)
        return (x, itok_B_0_15, itok_B_0_3)
    x, itok_B_0_15, itok_B_0_3 = _rec_inputs()

    def _L0_cond_setup():
        import jax, jax.numpy as jnp
        import numpy as np
        INPUT_DIM = 256
        OUTPUT_DIM = 256
        NUM_CATEGORIES = 16
        B, S = (32, 128)
        key = jax.random.key(seed)
        kx, kw, kb, ki = jax.random.split(key, 4)
        k = 1.0 / np.sqrt(INPUT_DIM)
        x = jax.random.normal(kx, (B, S, INPUT_DIM), dtype=jnp.float32)
        weight = jax.random.uniform(kw, (NUM_CATEGORIES, INPUT_DIM, OUTPUT_DIM), dtype=jnp.float32, minval=-k, maxval=k)
        bias = jax.random.uniform(kb, (NUM_CATEGORIES, OUTPUT_DIM), dtype=jnp.float32, minval=-k, maxval=k)
        emb_ids = jax.random.randint(ki, (B,), 0, NUM_CATEGORIES, dtype=jnp.int64)
        return {'x': x, 'emb_ids': emb_ids, 'weight': weight, 'bias': bias}
    _L0_cond_all = _L0_cond_setup()
    _L0_cond_in = {k: v for k, v in _L0_cond_all.items() if k in ('weight', 'bias')}
    del _L0_cond_all

    def _L0_attn_setup():
        import jax, jax.numpy as jnp
        import numpy as np
        EMBED_DIM = 256
        NUM_HEADS = 16
        HEAD_DIM = EMBED_DIM // NUM_HEADS
        LORA_R = 8
        ALPHA = 1.0
        B, S = (2, 512)

        def lora_linear(x, W, b, A, Bm):
            return x @ W.T + b + x @ A.T @ Bm.T * (ALPHA / LORA_R)
        key = jax.random.key(seed)
        ks = jax.random.split(key, 20)
        d = {'x': jax.random.normal(ks[0], (B, S, EMBED_DIM), dtype=jnp.float32)}
        names = ['q', 'k', 'v', 'o']
        i = 1
        for n in names:
            d['W' + n] = jax.random.normal(ks[i], (EMBED_DIM, EMBED_DIM), jnp.float32) * 0.02
            i += 1
            d['b' + n] = jnp.zeros((EMBED_DIM,), jnp.float32)
            d['A' + n] = jax.random.normal(ks[i], (LORA_R, EMBED_DIM), jnp.float32) * 0.02
            i += 1
            d['B' + n] = jax.random.normal(ks[i], (EMBED_DIM, LORA_R), jnp.float32) * 0.02
            i += 1
        d['rezero'] = jnp.zeros((1,), jnp.float32) + 0.1
        return d
    _L0_attn_all = _L0_attn_setup()
    _L0_attn_in = {k: v for k, v in _L0_attn_all.items() if k in ('Wq', 'bq', 'Aq', 'Bq', 'Wk', 'bk', 'Ak', 'Bk', 'Wv', 'bv', 'Av', 'Bv', 'Wo', 'bo', 'Ao', 'Bo', 'rezero')}
    del _L0_attn_all

    def _L0_cond2_setup():
        import jax, jax.numpy as jnp
        import numpy as np
        D = 256
        RANK = 16
        ALPHA = 16.0
        SCALING = ALPHA / RANK
        N_LANG = 4
        B, S = (32, 512)
        key = jax.random.key(seed)
        k1, k2, k3, k4, k5 = jax.random.split(key, 5)
        x = jax.random.normal(k1, (B, S, D), dtype=jnp.float32)
        language_ids = jax.random.randint(k2, (B,), 0, N_LANG, dtype=jnp.int32)
        lora_A = jax.random.normal(k3, (N_LANG, RANK, D), dtype=jnp.float32) * 0.02
        lora_B = jax.random.normal(k4, (N_LANG, D, RANK), dtype=jnp.float32) * 0.02
        lang_embed = jax.random.normal(k5, (N_LANG, D), dtype=jnp.float32) * 0.02
        return {'x': x, 'language_ids': language_ids, 'lora_A': lora_A, 'lora_B': lora_B, 'lang_embed': lang_embed}
    _L0_cond2_all = _L0_cond2_setup()
    _L0_cond2_in = {k: v for k, v in _L0_cond2_all.items() if k in ('lora_A', 'lora_B', 'lang_embed')}
    del _L0_cond2_all

    def _L0_ffn_setup():
        import jax, jax.numpy as jnp
        import numpy as np
        D = 256
        E = 12
        HS = 2 * D
        HR = 3 * D
        TAU = 1.5

        def _geglu(h):
            a, g = jnp.split(h, 2, axis=-1)
            return a * jax.nn.gelu(g, approximate=False)
        key = jax.random.key(seed)
        ks = jax.random.split(key, 12)

        def xavier(k, shape):
            fan_in, fan_out = (shape[-2], shape[-1])
            lim = jnp.sqrt(6.0 / (fan_in + fan_out))
            return jax.random.uniform(k, shape, jnp.float32, -lim, lim)
        x = jax.random.normal(ks[0], (2, 256, D), jnp.float32)
        Ws1 = xavier(ks[1], (D, 2 * HS))
        bs1 = jnp.zeros((2 * HS,), jnp.float32)
        Ws2 = xavier(ks[2], (HS, D))
        bs2 = jnp.zeros((D,), jnp.float32)
        We1 = xavier(ks[3], (E, D, 2 * HR))
        be1 = jnp.zeros((E, 2 * HR), jnp.float32)
        We2 = xavier(ks[4], (E, HR, D))
        be2 = jnp.zeros((E, D), jnp.float32)
        Wr = xavier(ks[5], (D, E))
        br = jnp.zeros((E,), jnp.float32)
        return {'x': x, 'Ws1': Ws1, 'bs1': bs1, 'Ws2': Ws2, 'bs2': bs2, 'We1': We1, 'be1': be1, 'We2': We2, 'be2': be2, 'Wr': Wr, 'br': br}
    _L0_ffn_all = _L0_ffn_setup()
    _L0_ffn_in = {k: v for k, v in _L0_ffn_all.items() if k in ('Ws1', 'bs1', 'Ws2', 'bs2', 'We1', 'be1', 'We2', 'be2', 'Wr', 'br')}
    del _L0_ffn_all
    return {'x': x, 'itok_B_0_15': itok_B_0_15, 'itok_B_0_3': itok_B_0_3, 'L0_cond_weight': _L0_cond_in['weight'], 'L0_cond_bias': _L0_cond_in['bias'], 'L0_attn_Wq': _L0_attn_in['Wq'], 'L0_attn_bq': _L0_attn_in['bq'], 'L0_attn_Aq': _L0_attn_in['Aq'], 'L0_attn_Bq': _L0_attn_in['Bq'], 'L0_attn_Wk': _L0_attn_in['Wk'], 'L0_attn_bk': _L0_attn_in['bk'], 'L0_attn_Ak': _L0_attn_in['Ak'], 'L0_attn_Bk': _L0_attn_in['Bk'], 'L0_attn_Wv': _L0_attn_in['Wv'], 'L0_attn_bv': _L0_attn_in['bv'], 'L0_attn_Av': _L0_attn_in['Av'], 'L0_attn_Bv': _L0_attn_in['Bv'], 'L0_attn_Wo': _L0_attn_in['Wo'], 'L0_attn_bo': _L0_attn_in['bo'], 'L0_attn_Ao': _L0_attn_in['Ao'], 'L0_attn_Bo': _L0_attn_in['Bo'], 'L0_attn_rezero': _L0_attn_in['rezero'], 'L0_cond2_lora_A': _L0_cond2_in['lora_A'], 'L0_cond2_lora_B': _L0_cond2_in['lora_B'], 'L0_cond2_lang_embed': _L0_cond2_in['lang_embed'], 'L0_ffn_Ws1': _L0_ffn_in['Ws1'], 'L0_ffn_bs1': _L0_ffn_in['bs1'], 'L0_ffn_Ws2': _L0_ffn_in['Ws2'], 'L0_ffn_bs2': _L0_ffn_in['bs2'], 'L0_ffn_We1': _L0_ffn_in['We1'], 'L0_ffn_be1': _L0_ffn_in['be1'], 'L0_ffn_We2': _L0_ffn_in['We2'], 'L0_ffn_be2': _L0_ffn_in['be2'], 'L0_ffn_Wr': _L0_ffn_in['Wr'], 'L0_ffn_br': _L0_ffn_in['br']}

def reference(x, itok_B_0_15, itok_B_0_3, L0_cond_weight, L0_cond_bias, L0_attn_Wq, L0_attn_bq, L0_attn_Aq, L0_attn_Bq, L0_attn_Wk, L0_attn_bk, L0_attn_Ak, L0_attn_Bk, L0_attn_Wv, L0_attn_bv, L0_attn_Av, L0_attn_Bv, L0_attn_Wo, L0_attn_bo, L0_attn_Ao, L0_attn_Bo, L0_attn_rezero, L0_cond2_lora_A, L0_cond2_lora_B, L0_cond2_lang_embed, L0_ffn_Ws1, L0_ffn_bs1, L0_ffn_Ws2, L0_ffn_bs2, L0_ffn_We1, L0_ffn_be1, L0_ffn_We2, L0_ffn_be2, L0_ffn_Wr, L0_ffn_br):
    import jax
    import jax.numpy as jnp

    def _L0_cond_ref(x, emb_ids, weight, bias):
        import jax, jax.numpy as jnp
        import numpy as np
        INPUT_DIM = 256
        OUTPUT_DIM = 256
        NUM_CATEGORIES = 16
        B, S = (32, 128)
        ids = emb_ids.reshape(-1).astype(jnp.int32)
        w = weight[ids]
        b = bias[ids]
        return jnp.einsum('bsi,bij->bsj', x, w) + b[:, None, :]

    def _L0_attn_ref(x, Wq, bq, Aq, Bq, Wk, bk, Ak, Bk, Wv, bv, Av, Bv, Wo, bo, Ao, Bo, rezero):
        import jax, jax.numpy as jnp
        import numpy as np
        EMBED_DIM = 256
        NUM_HEADS = 16
        HEAD_DIM = EMBED_DIM // NUM_HEADS
        LORA_R = 8
        ALPHA = 1.0
        B, S = (2, 512)

        def lora_linear(x, W, b, A, Bm):
            return x @ W.T + b + x @ A.T @ Bm.T * (ALPHA / LORA_R)
        bsz, seq_len, _ = x.shape
        Q = lora_linear(x, Wq, bq, Aq, Bq).reshape(bsz, seq_len, NUM_HEADS, HEAD_DIM)
        K = lora_linear(x, Wk, bk, Ak, Bk).reshape(bsz, seq_len, NUM_HEADS, HEAD_DIM)
        V = lora_linear(x, Wv, bv, Av, Bv).reshape(bsz, seq_len, NUM_HEADS, HEAD_DIM)
        scores = jnp.einsum('bqhd,bkhd->bhqk', Q, K) / np.sqrt(HEAD_DIM).astype(np.float32)
        slopes = 0.5 ** jnp.arange(NUM_HEADS, dtype=jnp.float32)
        pos = jnp.arange(seq_len, dtype=jnp.float32)
        rel = pos[None, :] - pos[:, None]
        scores = scores + slopes[None, :, None, None] * rel[None, None, :, :]
        attn = jax.nn.softmax(scores, axis=-1)
        out = jnp.einsum('bhqk,bkhd->bqhd', attn, V).reshape(bsz, seq_len, EMBED_DIM)
        out = lora_linear(out, Wo, bo, Ao, Bo)
        return x + rezero * out

    def _L0_cond2_ref(x, language_ids, lora_A, lora_B, lang_embed):
        import jax, jax.numpy as jnp
        import numpy as np
        D = 256
        RANK = 16
        ALPHA = 16.0
        SCALING = ALPHA / RANK
        N_LANG = 4
        B, S = (32, 512)
        A = lora_A[language_ids]
        Bm = lora_B[language_ids]
        emb = lang_embed[language_ids]
        t = jnp.einsum('bsd,brd->bsr', x, A)
        lora_out = jnp.einsum('bsr,bdr->bsd', t, Bm) * SCALING
        return lora_out + emb[:, None, :]

    def _L0_ffn_ref(x, Ws1, bs1, Ws2, bs2, We1, be1, We2, be2, Wr, br):
        import jax, jax.numpy as jnp
        import numpy as np
        D = 256
        E = 12
        HS = 2 * D
        HR = 3 * D
        TAU = 1.5

        def _geglu(h):
            a, g = jnp.split(h, 2, axis=-1)
            return a * jax.nn.gelu(g, approximate=False)
        B, T, Dm = x.shape
        xf = x.reshape(-1, Dm)
        ys = _geglu(xf @ Ws1 + bs1) @ Ws2 + bs2
        logits = (xf @ Wr + br) / TAU
        top_val, top_idx = jax.lax.top_k(logits, 2)
        top_w = jax.nn.softmax(top_val, axis=-1)
        onehot = jax.nn.one_hot(top_idx, E, dtype=x.dtype)
        w = jnp.einsum('nke,nk->ne', onehot, top_w)
        h = jnp.einsum('nd,edh->enh', xf, We1) + be1[:, None, :]
        act = _geglu(h)
        yE = jnp.einsum('enh,ehd->end', act, We2) + be2[:, None, :]
        yr = jnp.einsum('end,ne->nd', yE, w)
        return (ys + yr).reshape(B, T, Dm)
    x = x + _L0_attn_ref(_L0_cond_ref(x, itok_B_0_15, L0_cond_weight, L0_cond_bias), L0_attn_Wq, L0_attn_bq, L0_attn_Aq, L0_attn_Bq, L0_attn_Wk, L0_attn_bk, L0_attn_Ak, L0_attn_Bk, L0_attn_Wv, L0_attn_bv, L0_attn_Av, L0_attn_Bv, L0_attn_Wo, L0_attn_bo, L0_attn_Ao, L0_attn_Bo, L0_attn_rezero)
    x = x + _L0_ffn_ref(_L0_cond2_ref(x, itok_B_0_3, L0_cond2_lora_A, L0_cond2_lora_B, L0_cond2_lang_embed), L0_ffn_Ws1, L0_ffn_bs1, L0_ffn_Ws2, L0_ffn_bs2, L0_ffn_We1, L0_ffn_be1, L0_ffn_We2, L0_ffn_be2, L0_ffn_Wr, L0_ffn_br)
    return x

_drawn_inputs = setup_inputs


def setup_inputs(seed=0):
    import zlib

    import numpy as np

    out = dict(_drawn_inputs(seed))
    spreads = {'L0_attn_bq': (0.0, 0.8),
     'L0_attn_bk': (0.0, 2.0),
     'L0_attn_bv': (0.0, 0.8),
     'L0_attn_bo': (0.0, 0.8),
     'L0_ffn_bs1': (0.0, 0.8),
     'L0_ffn_bs2': (0.0, 0.38),
     'L0_ffn_be1': (0.0, 0.8),
     'L0_ffn_be2': (0.0, 0.534),
     'L0_ffn_br': (0.0, 0.1)}
    factors = {'L0_attn_Wq': 8.0,
     'L0_attn_Aq': 8.0,
     'L0_attn_Bq': 8.0,
     'L0_attn_Wk': 8.0,
     'L0_attn_Ak': 8.0,
     'L0_attn_Bk': 8.0,
     'L0_attn_Wv': 8.0,
     'L0_attn_Av': 8.0,
     'L0_attn_Bv': 8.0,
     'L0_attn_Wo': 8.0,
     'L0_attn_Ao': 8.0,
     'L0_attn_Bo': 8.0,
     'L0_ffn_Ws1': 8.0,
     'L0_ffn_Ws2': 8.0,
     'L0_ffn_We1': 8.0,
     'L0_ffn_We2': 8.0}
    for name, (base, spread) in spreads.items():
        noise = np.random.default_rng([zlib.crc32(name.encode()), seed]).standard_normal(out[name].shape)
        drawn = base * np.exp(spread * noise) if base else spread * noise
        out[name] = jnp.asarray(drawn.astype(out[name].dtype))
    for name, factor in factors.items():
        out[name] = (out[name] * factor).astype(out[name].dtype)
    return out
```

```python
import numpy as np
import concourse.bass as bass
from concourse import mybir
from contextlib import ExitStack

P = 128
B, S, D = 64, 64, 256
H, HD = 16, 16
NCAT, NLANG, RANK, LR = 16, 4, 16, 8
NE, HR, HS = 12, 768, 512
TAU = 1.5
TOK = B * S
NT = TOK // P
KC = D // P
NLR = NLANG * RANK
TW = NLR + NLANG + 1
TWP = 72
NS = (2 * TOK + NE * (P - 1)) // P
CH = 256
NJ = HR // CH
EW = 2 * HR
E2 = HR // P * D
NEG = -3.0e38
CONST_COLS = dict(ident=P, tri=P, kmask=2, kv=2, count_down=NE, tile_start=NT, slot_tile=NS, part=1)


def adaln_attn_moe(nc, args, out):
    f32, bf16, i32, u32 = mybir.dt.float32, mybir.dt.bfloat16, mybir.dt.int32, mybir.dt.uint32
    ALU, ACT, AX = mybir.AluOpType, mybir.ActivationFunctionType, mybir.AxisListType
    ds = bass.ds
    a = args
    x_rows = a["x"].rearrange("b s d -> (b s) d")
    out_rows = out.rearrange("b s d -> (b s) d")
    cond_w_dram = a["L0_cond_weight"].rearrange("k (c p) n -> k p c n", p=P)

    ctx = ExitStack()
    with ctx:
        def sb(name, shape, dt=f32):
            return ctx.enter_context(nc.sbuf_tensor(name, shape, dt))

        def sem(name):
            return ctx.enter_context(nc.semaphore(name))

        x2_dram = nc.dram_tensor("x2_dram", [TOK, D], f32).ap()
        slot_rows = nc.dram_tensor("slot_rows", [NS * P, TWP], f32).ap()
        slot_out = nc.dram_tensor("slot_out", [NS * P, D], f32).ap()

        consts = sb("consts", [P, sum(CONST_COLS.values())])
        col, at = {}, 0
        for name, n in CONST_COLS.items():
            col[name] = consts[:, at:at + n]
            at += n
        ident = col["ident"]
        w1m = sb("w1_merged", [P, NE * EW + 2 * HS])
        lrows = sb("token_rows", [P, NT, TWP])
        ltT = sb("token_rows_T", [P, TOK])
        logits = sb("logits", [P, NT, NE])
        gate = sb("gate", [P, 2, NT])
        slot = sb("slot", [P, 2, NT], u32)
        expert_of = sb("expert_of", [1, NS], i32)
        be2_bc = sb("be2_bc", [P, NE * D])
        stage = sb("stage", [P, NJ * 1024])
        bs2_bc = sb("bs2_bc", [P, D])
        arena = sb("arena", [P, NE * E2 + HS // P * D])

        class Cut:
            def __init__(self, tensor):
                self.tensor, self.at = tensor, 0
                self.flat = tensor[:, :] if len(tensor.shape) == 2 else tensor[:, :, :].rearrange("p a b -> p (a b)")

            def __call__(self, *shape, parts=P):
                n = 1
                for s in shape:
                    n *= s
                ap = self.flat[0:parts, self.at:self.at + n]
                self.at += n
                assert self.at <= self.flat.shape[1]
                if len(shape) == 1:
                    return ap
                names = "abcde"[:len(shape)]
                dims = {k: v for k, v in zip(names, shape)}
                return ap.rearrange(f"p ({' '.join(names)}) -> p {' '.join(names)}", **dims)

        cut = Cut(arena)
        x_in = [cut(D) for _ in range(2)]
        x_bo = [cut(D) for _ in range(2)]
        cond_w = [cut(2, KC, D) for _ in range(2)]
        xT = cut(KC, P)
        cT = [cut(KC, P) for _ in range(2)]
        qT = cut(KC, P)
        kD = cut(KC, 2, P)
        vD = [cut(2, 8, 34) for _ in range(2)]
        probs = cut(1024)
        probsT = cut(8, P)
        onorm = cut(D)
        oT = cut(KC, P)
        x2 = [cut(D) for _ in range(2)]
        x2T = cut(KC, P)
        trow = cut(TWP)
        trowT = cut(P)
        smax = cut(H)
        rsum = cut(H)
        wm = [cut(KC, D) for _ in range(4)]
        w_raw = [cut(KC, D) for _ in range(4)]
        a_raw = [cut(D, parts=LR) for _ in range(4)]
        b_raw = [cut(KC, LR) for _ in range(4)]
        bT = cut(4, D, parts=LR)
        lora_a = cut(D, parts=NLR)
        aT = cut(KC, NLR)
        cond_b = cut(D, parts=NCAT)
        cat_hot = cut(B, parts=NCAT)
        cond_bT = cut(B, KC)
        bq_col, bk_col, bq_quarter, rz = cut(KC), cut(KC), cut(KC), cut(1)
        bv_half = cut(P)
        bo_bc, bo_rz = cut(D), cut(D)
        wr_raw = cut(KC, NE)
        wr = cut(NE)
        lang_f = cut(NT)
        lang_hot = cut(NT, NLANG)
        cat_f = cut(B, parts=NCAT)
        ali_f = cut(P + H * S, parts=2)
        ali = cut((P + H * S) // 2, parts=2).bitcast(bf16)
        ba = sb("ba", [P, KC, NLR + NLANG])
        cat_i = sb("cat_i", [1, B], i32)
        cat16_i = sb("cat16_i", [NCAT, B], i32)
        lang_i = sb("lang_i", [P, NT], i32)
        tri_b = sb("tri_b", [P, P], bf16)
        ones_b = sb("ones_b", [P, P], bf16)
        cut = Cut(be2_bc)
        r_a, r_b, r_m1, r_m2 = [cut(NT, NE) for _ in range(4)]
        r_max1, r_max2, r_s, r_d = [cut(NT) for _ in range(4)]
        r_n, r_tiles, r_end, r_base, r_one = [cut(NE) for _ in range(5)]
        r_et = cut(NS, NE)
        r_cmp = r_et.rearrange("p t e -> p (t e)")[:, 0:NE * NT].rearrange("p (e t) -> p e t", e=NE)
        r_ef = cut(NS)
        chosen = cut(NT * NE // 2).bitcast(bf16)
        cut = Cut(stage)
        stage_w = [stage[:, j * 1024:(j + 1) * 1024].rearrange("p (c n) -> p c n", c=KC) for j in range(NJ)]
        s_row = [cut(TWP) for _ in range(3)]
        s_rowT = [cut(P) for _ in range(3)]
        g_sb = [cut(CH) for _ in range(2)]
        act_sb = [cut(CH) for _ in range(3)]
        y_sb = [cut(D) for _ in range(2)]
        cut = Cut(lrows)
        y_sb.append(cut(D))
        g_sb.append(cut(CH))
        actT_sb = [cut(2, P) for _ in range(3)]
        cut = Cut(arena)
        sh_g = [cut(512) for _ in range(2)]
        sh_aT = [cut(HS // P, 512) for _ in range(2)]
        c_x2 = [cut(D) for _ in range(4)]
        c_y = [cut(2, D) for _ in range(4)]
        c_out = [cut(D) for _ in range(4)]
        ws2 = arena[:, NE * E2:].rearrange("p (k n) -> p k n", n=D)

        ps = ctx.enter_context(nc.psum_tensor("ps", [P, 8, 512], f32))

        d_setup, d_w1bias, d_zero = sem("d_setup"), sem("d_w1bias"), sem("d_zero")
        d_x = [sem(f"d_x{s}") for s in range(2)]
        d_cw = [sem(f"d_cw{s}") for s in range(2)]
        d_x2 = [sem(f"d_x2{s}") for s in range(2)]
        s_const, s_hot, s_sp1, s_sp1c, s_bT, s_mrg, s_mrgc = [sem(n) for n in (
            "s_const", "s_hot", "s_sp1", "s_sp1c", "s_bT", "s_mrg", "s_mrgc")]
        s_zero = sem("s_zero")
        chain = sem("chain")
        (xT_ps, xT_sb, cT_ps, cT_sb, xbo_sb, q_ps, q_sb, k_ps, k_sb, v_ps, v_sb, s_ps, max_sb, shift_sb,
         prob_sb, pT_ps, pTa_sb, pTv_sb, o_ps, rsum_sb, o_sb, oT_ps, oT_sb, att_ps, x2_sb, x2T_ps, x2T_sb,
         t_ps, t_sb, tT_ps, tT_sb, lg_ps, lg_sb, kept_t, kept_tT) = [sem(n) for n in (
             "xT_ps xT_sb cT_ps cT_sb xbo_sb q_ps q_sb k_ps k_sb v_ps v_sb s_ps max_sb shift_sb "
             "prob_sb pT_ps pTa_sb pTv_sb o_ps rsum_sb o_sb oT_ps oT_sb att_ps x2_sb x2T_ps x2T_sb "
             "t_ps t_sb tT_ps tT_sb lg_ps lg_sb kept_t kept_tT").split()]
        d_stage = [sem(f"d_stage{j}") for j in range(NJ)]
        d_w2, d_be2, d_scatter = sem("d_w2"), sem("d_be2"), sem("d_scatter")
        merge_ps, merge_sb, r_gap, r_exp, r_chosen, r_rank, r_slots, r_done = [sem(n) for n in (
            "merge_ps", "merge_sb", "r_gap", "r_exp", "r_chosen", "r_rank", "r_slots", "r_done")]
        d_row = [sem(f"d_row{s}") for s in range(3)]
        d_y = [sem(f"d_y{s}") for s in range(3)]
        (rowT_ps, rowT_sb, h_ps, g_ok, act_ok, actT_ps, actT_ok, y_ps, y_ok) = [sem(n) for n in (
            "rowT_ps", "rowT_sb", "h_ps", "g_ok", "act_ok", "actT_ps", "actT_ok", "y_ps", "y_ok")]
        d_cx = [sem(f"d_cx{s}") for s in range(4)]
        d_cy = [sem(f"d_cy{s}") for s in range(4)]
        d_out = [sem(f"d_out{s}") for s in range(4)]
        sh_ps, shg_ok, sha_ok, shy_ps, comb_ok = [sem(n) for n in (
            "sh_ps", "shg_ok", "sha_ok", "shy_ps", "comb_ok")]

        names = "qkvo"
        loads = [(consts[:, :], a["consts"]), (ali_f, a["alibi"])]
        for n, c in enumerate(names):
            loads += [(w_raw[n], a[f"L0_attn_W{c}"].rearrange("(m p) n -> p m n", p=P)),
                      (a_raw[n], a[f"L0_attn_A{c}"]),
                      (b_raw[n], a[f"L0_attn_B{c}"].rearrange("(m p) n -> p m n", p=P))]
        loads += [
            (lora_a, a["L0_cond2_lora_A"].rearrange("l r d -> (l r) d")),
            (cond_b, a["L0_cond_bias"]),
            (cat_i[:, :], a["itok_B_0_15"].unsqueeze(0)),
            (cat16_i[:, :], a["itok_B_0_15"].partition_broadcast(NCAT)),
            (bq_col, a["L0_attn_bq"].rearrange("(m p) -> p m", p=P)),
            (bk_col, a["L0_attn_bk"].rearrange("(m p) -> p m", p=P)),
            (rz, a["L0_attn_rezero"].partition_broadcast(P)),
            (bo_bc, a["L0_attn_bo"].partition_broadcast(P)),
            (bs2_bc[:, :], a["L0_ffn_bs2"].partition_broadcast(P)),
            (wr_raw, a["L0_ffn_Wr"].rearrange("(c p) n -> p c n", p=P)),
            (wr[TW - 1:TW, :], a["L0_ffn_br"].unsqueeze(0)),
        ]
        for c in range(KC):
            loads.append((ba[:, c, NLR:NLR + NLANG],
                          a["L0_cond2_lang_embed"][:, c * P:(c + 1) * P].rearrange("l p -> p l")))
            for lang in range(NLANG):
                loads.append((ba[:, c, lang * RANK:(lang + 1) * RANK],
                              a["L0_cond2_lora_B"][lang, c * P:(c + 1) * P, :]))
        for h in range(2):
            loads.append((bv_half[h * S:(h + 1) * S, :].rearrange("p (h d) -> p h d", d=HD),
                          a["L0_attn_bv"].rearrange("(h two d) -> two h d", two=2, d=HD)[h].partition_broadcast(S)))
            loads.append((lang_i[h * S:(h + 1) * S, :],
                          a["itok_B_0_3"].rearrange("(t two) -> two t", two=2)[h].partition_broadcast(S)))
        ALL_SETUP = 16 * len(loads)
        be1_rows = [(w1m[TW - 1:TW, 0:NE * EW].rearrange("p (e j g n) -> p g e j n", e=NE, j=NJ, g=2)[:, g],
                     a["L0_ffn_be1"][:, g * HR:(g + 1) * HR].rearrange("e (j n) -> e j n", j=NJ).unsqueeze(0))
                    for g in range(2)]
        be1_rows += [(w1m[TW - 1:TW, NE * EW:].rearrange("p (j g n) -> p g j n", j=HS // CH, g=2)[:, g],
                      a["L0_ffn_bs1"][g * HS:(g + 1) * HS].rearrange("(j n) -> j n", n=CH).unsqueeze(0))
                     for g in range(2)]

        def turn(i, odd):
            return 8 * i + (8 if odd else 16)

        def w1_cols(e, j):
            return ds(e * EW + j * 2 * CH, 2 * CH)

        n_merge = NE * NJ + HS // CH

        block = ctx.enter_context(nc.Block())

        @block.sync
        def _(sp):
            for dst, src in loads:
                with nc.allow_non_contiguous_dma(reason="a few hundred words of biases, embeddings and ids"):
                    sp.dma_start(dst, src).then_inc(d_setup, 16)
            for dst, src in be1_rows:
                sp.dma_start(dst, src).then_inc(d_w1bias, 16)
            sp.wait_ge(d_setup, ALL_SETUP)

            def load_tile(i, odd):
                s = int(odd)
                if not (isinstance(i, int) and i < 2):
                    sp.wait_ge(xT_ps, i - 1)
                    sp.wait_ge(xbo_sb, i - 1)
                    sp.wait_ge(cT_ps, i - 1)
                sp.dma_start(x_in[s], x_rows[ds(i * P, P), :]).then_inc(d_x[s], 16)
                for b in range(2):
                    cat = sp.value_load(cat_i[0:1, ds(i * 2 + b, 1)], min_val=0, max_val=NCAT - 1)
                    sp.dma_start(cond_w[s][:, b], cond_w_dram[ds(cat, 1), :, :, :].rearrange(
                        "o p c n -> p (o c) n")).then_inc(d_cw[s], 16)

            def store_x2(i, odd):
                sp.wait_ge(x2_sb, i + 1)
                sp.dma_start(x2_dram[ds(i * P, P), :], x2[int(odd)]).then_inc(d_x2[int(odd)], 16)

            load_tile(0, False)
            load_tile(1, True)
            load_tile(2, False)
            with sp.Fori(1, NT - 4, 2) as i:
                load_tile(i + 2, True)
                store_x2(i - 1, False)
                load_tile(i + 3, False)
                store_x2(i, True)
            load_tile(NT - 1, True)
            for i in range(NT - 4, NT):
                store_x2(i, i % 2 == 1)

            def load_first(j, src):
                for c in range(KC):
                    sp.dma_start(stage_w[j][:, c, :].rearrange("p (g n) -> p g n", g=2),
                                 src[c * P:(c + 1) * P].rearrange("p (g n) -> p g n", g=2)[
                                     :, :, j * CH:(j + 1) * CH]).then_inc(d_stage[j], 16)

            def load_second(e):
                src = a["L0_ffn_We2"][ds(e, 1), :, :].rearrange("o (k p) n -> p (o k) n", p=P)
                sp.dma_start(arena[:, ds(e * E2, E2)].rearrange("p (k n) -> p k n", n=D), src).then_inc(d_w2, 16)

            def first_of(e):
                return a["L0_ffn_We1"][ds(e, 1), :, :].rearrange("o d n -> (o d) n")

            for j in range(NJ):
                load_first(j, first_of(0))
            sp.wait_ge(lg_sb, NT)
            sp.wait_ge(kept_t, NT)
            sp.wait_ge(kept_tT, NT)
            for s in range(2):
                sp.wait_ge(d_x2[s], 16 * NT // 2)
            load_second(0)
            with sp.Fori(1, NE) as e:
                for j in range(NJ):
                    sp.wait_ge(merge_ps, 3 * e + (j - 2))
                    load_first(j, first_of(e))
                load_second(e)
            for j in range(HS // CH):
                sp.wait_ge(merge_ps, NE * NJ - 2 + j)
                load_first(j, a["L0_ffn_Ws1"])
            sp.dma_start(ws2, a["L0_ffn_Ws2"].rearrange("(k p) n -> p k n", p=P)).then_inc(d_w2, 16)
            sp.wait_ge(r_done, 1)
            sp.dma_start(be2_bc[:, :], a["L0_ffn_be2"].rearrange("e n -> (e n)").partition_broadcast(P)
                         ).then_inc(d_be2, 16)

            def load_rows(t, s):
                if not (isinstance(t, int) and t < 3):
                    sp.wait_ge(rowT_ps, t - 2)
                sp.dma_start(s_row[s], slot_rows[ds(t * P, P), :]).then_inc(d_row[s], 16)

            def store_y(t, s):
                sp.wait_ge(y_ok, t + 1)
                sp.dma_start(slot_out[ds(t * P, P), :], y_sb[s]).then_inc(d_y[s], 16)

            sp.wait_ge(d_scatter, 16 * 2 * NT)
            sp.wait_ge(merge_ps, n_merge)
            load_rows(0, 0)
            load_rows(1, 1)
            load_rows(2, 2)
            with sp.Fori(1, NS // 3) as q:
                for s in range(3):
                    load_rows(3 * q + s, s)
                    store_y(3 * q + (s - 3), s)
            for t in range(NS - 3, NS):
                store_y(t, t % 3)

            def load_x2(n, v):
                if not (isinstance(n, int) and n < 4):
                    sp.wait_ge(comb_ok, n - 3)
                sp.dma_start(c_x2[v], x2_dram[ds(n * P, P), :]).then_inc(d_cx[v], 16)

            def store_out(n, v):
                sp.wait_ge(comb_ok, n + 1)
                sp.dma_start(out_rows[ds(n * P, P), :], c_out[v]).then_inc(d_out[v], 16)

            for v in range(4):
                load_x2(v, v)
            with sp.Fori(1, NT // 4) as u:
                for v in range(4):
                    load_x2(4 * u + v, v)
                    store_out(4 * u + (v - 4), v)
            for v in range(4):
                store_out(NT - 4 + v, v)
            for v in range(4):
                sp.wait_ge(d_out[v], 16 * NT // 4)

        @block.gpsimd
        def _(pool):
            zeros = lrows[:, 0, :]
            nc.gpsimd.memset(zeros, 0.0).then_inc(s_zero, 1)
            for s in range(2):
                nc.gpsimd.memset(vD[s], 0.0).then_inc(s_zero, 1)
            nc.gpsimd.memset(ones_b[:, :], 1.0).then_inc(s_zero, 1)
            nc.gpsimd.memset(trow, 1.0).then_inc(s_zero, 1)
            pool.wait_ge(s_zero, 1)
            pool.dma_start(slot_rows.rearrange("(t p) n -> p t n", p=P),
                           zeros.unsqueeze(1).to_broadcast([P, NS, TWP])).then_inc(d_zero, 16)
            pool.wait_ge(d_zero, 16)
            nc.gpsimd.memset(lrows[:, :, NLR:TWP], 0.0).then_inc(s_zero, 1)
            pool.wait_ge(s_zero, 6)
            nc.gpsimd.memset(lrows[:, :, TW - 1:TW], 1.0).then_inc(s_zero, 1)
            pool.wait_ge(s_hot, 1)
            nc.gpsimd.tensor_copy(lrows[:, :, NLR:NLR + NLANG], lang_hot).then_inc(s_zero, 1)

            def residual(i, odd):
                s = int(odd)
                pool.wait_ge(d_x[s], turn(i, odd))
                if not (isinstance(i, int) and i < 2):
                    pool.wait_ge(x2_sb, i - 1)
                nc.gpsimd.tensor_tensor(x_bo[s], x_in[s], bo_rz, ALU.add).then_inc(xbo_sb, 1)

            def keep(i):
                pool.wait_ge(t_sb, i + 1)
                nc.gpsimd.tensor_copy(lrows[:, ds(i, 1), 0:NLR].rearrange("p o n -> p (o n)"),
                                      trow[:, 0:NLR]).then_inc(kept_t, 1)
                pool.wait_ge(tT_sb, i + 1)
                nc.gpsimd.tensor_copy(ltT[0:TW, ds(i * P, P)], trowT[0:TW, :]).then_inc(kept_tT, 1)

            pool.wait_ge(s_hot, 1)
            residual(0, False)
            residual(1, True)
            with pool.Fori(1, NT - 2, 2) as i:
                residual(i + 1, False)
                keep(i - 1)
                residual(i + 2, True)
                keep(i)
            keep(NT - 2)
            keep(NT - 1)

            pool.wait_ge(r_slots, 2)
            pool.wait_ge(kept_t, NT)
            pool.wait_ge(s_zero, 8)
            for k in range(2):
                for i in range(NT):
                    pool.indirect_dma_start(slot_rows, bass.IndirectOffsetOnAxis(slot[:, k, i:i + 1], 0),
                                            lrows[:, i, :], None).then_inc(d_scatter, 16)

            for s in range(3):
                pool.wait_ge(d_y[s], 16 * NS // 3)
            for n in range(NT):
                if n >= 4:
                    pool.wait_ge(comb_ok, n - 3)
                for k in range(2):
                    pool.indirect_dma_start(c_y[n % 4][:, k, :], None, slot_out,
                                            bass.IndirectOffsetOnAxis(slot[:, k, n:n + 1], 0)
                                            ).then_inc(d_cy[n % 4], 16)

        @block.scalar
        def _(act):
            copy = nc.scalar.copy
            act.wait_ge(s_sp1, 1)
            copy(aT, ps[:, 0, 0:KC * NLR].rearrange("p (c n) -> p c n", c=KC))
            copy(wr[0:NLR + NLANG, :], ps[0:NLR + NLANG, 0, 256:256 + NE])
            copy(cond_bT.rearrange("p b m -> p m b"), ps[:, 1, 0:KC * B].rearrange("p (m b) -> p m b", m=KC)
                 ).then_inc(s_sp1c, 1)
            act.wait_ge(s_sp1, 2)
            nc.scalar.mul(bT, ps[0:LR, 2:4, :].rearrange("p t (n m) -> p (t n) m", m=D), 1.0 / LR).then_inc(s_bT, 1)
            for n in range(4):
                act.wait_ge(s_mrg, n + 1)
                src = ps[:, 4 + n, :].rearrange("p (c n) -> p c n", c=KC)
                if n < 3:
                    copy(wm[n], src).then_inc(s_mrgc, 1)
                else:
                    nc.scalar.activation(wm[n], src, ACT.Copy, scale=rz).then_inc(s_mrgc, 1)
            act.wait_ge(s_hot, 1)

            def xT_copy(i):
                act.wait_ge(xT_ps, i + 1)
                copy(xT, ps[:, 4, 0:D].rearrange("p (c n) -> p c n", c=KC)).then_inc(xT_sb, 1)

            def q_copy(i):
                act.wait_ge(q_ps, i + 1)
                for m in range(KC):
                    last = nc.scalar.activation(qT[:, m, :], ps[:, 5, m * P:(m + 1) * P], ACT.Identity,
                                                bias=bq_quarter[:, m:m + 1], scale=0.25)
                last.then_inc(q_sb, 1)

            def exps(i):
                act.wait_ge(shift_sb, i + 1)
                nc.scalar.activation(probs, probs, ACT.Exp).then_inc(prob_sb, 1)

            def pT_copy(i):
                act.wait_ge(pT_ps, 2 * i + 1)
                copy(probsT[:, 0:4, :].rearrange("p a n -> p (a n)"), ps[:, 0, :]).then_inc(pTa_sb, 1)

            def oT_copy(i):
                act.wait_ge(oT_ps, i + 1)
                copy(oT, ps[:, 7, 0:D].rearrange("p (c n) -> p c n", c=KC)).then_inc(oT_sb, 1)

            def x2T_copy(i):
                act.wait_ge(x2T_ps, i + 1)
                copy(x2T, ps[:, 7, 0:D].rearrange("p (c n) -> p c n", c=KC)).then_inc(x2T_sb, 1)

            def tT_copy(i):
                act.wait_ge(tT_ps, i + 1)
                if not isinstance(i, int) or i > 0:
                    act.wait_ge(kept_tT, i)
                copy(trowT[0:TW, :], ps[0:TW, 7, 0:P]).then_inc(tT_sb, 1)

            def tile_steps(i, first=False, last=False):
                if not last:
                    xT_copy(i + 1)
                if not first:
                    oT_copy(i - 1)
                    x2T_copy(i - 1)
                if not last:
                    q_copy(i + 1)
                exps(i)
                if not first:
                    tT_copy(i - 1)
                pT_copy(i)

            xT_copy(0)
            q_copy(0)
            tile_steps(0, first=True)
            tile_steps(1)
            tile_steps(2)
            with act.Fori(3, NT - 2, 2) as i:
                tile_steps(i)
                tile_steps(i + 1)
            tile_steps(NT - 1, last=True)
            oT_copy(NT - 1)
            x2T_copy(NT - 1)
            tT_copy(NT - 1)

            def merge_copy(n, j, dst):
                act.wait_ge(merge_ps, n + 1)
                copy(dst, ps[0:NLR + NLANG, 3 + j, :]).then_inc(merge_sb, 1)

            act.wait_ge(r_gap, 1)
            nc.scalar.activation(r_d, r_d, ACT.Exp).then_inc(r_exp, 1)
            with act.Fori(0, NE) as e:
                for j in range(NJ):
                    merge_copy(3 * e + j, j, w1m[0:NLR + NLANG, w1_cols(e, j)])
            for j in range(HS // CH):
                merge_copy(NE * NJ + j, j, w1m[0:NLR + NLANG, NE * EW + j * 2 * CH:NE * EW + (j + 1) * 2 * CH])

            def gelu(n, j):
                act.wait_ge(h_ps, n + 1)
                nc.scalar.activation(g_sb[j], ps[:, j, CH:2 * CH], ACT.Gelu).then_inc(g_ok, 1)

            def actT_copy(n, j):
                act.wait_ge(actT_ps, n + 1)
                copy(actT_sb[j], ps[:, 3 + j, 0:CH].rearrange("p (c n) -> p c n", c=2)).then_inc(actT_ok, 1)

            gelu(0, 0)
            with act.Fori(0, NS - 1) as t:
                for j in range(NJ):
                    gelu(3 * t + (j + 1), (j + 1) % NJ)
                    actT_copy(3 * t + j, j)
            for j in range(NJ):
                if j < NJ - 1:
                    gelu(3 * (NS - 1) + j + 1, j + 1)
                actT_copy(3 * (NS - 1) + j, j)

            with act.Fori(0, NT // 4) as u:
                for c in range(4):
                    act.wait_ge(sh_ps, 4 * u + (c + 1))
                    nc.scalar.activation(sh_g[c % 2], ps[:, 2 * (c % 2) + 1, :], ACT.Gelu).then_inc(shg_ok, 1)

        @block.vector
        def _(dve):
            links = [0]

            def link(ins):
                links[0] += 1
                ins.then_inc(chain, 1)
                dve.wait_ge(chain, links[0])

            V = nc.vector
            dve.wait_ge(d_setup, ALL_SETUP)
            V.tensor_copy(ali, ali_f).then_inc(s_const, 1)
            V.tensor_copy(tri_b[:, :], col["tri"]).then_inc(s_const, 1)
            link(V.tensor_copy(cat_f, cat16_i[:, :]))
            V.tensor_scalar(cat_hot, cat_f, col["part"][0:NCAT, :], None, ALU.is_equal).then_inc(s_const, 1)
            link(V.tensor_copy(lang_f, lang_i[:, :]))
            for lang in range(NLANG):
                V.tensor_scalar(lang_hot[:, :, lang], lang_f, float(lang), None, ALU.is_equal)
            dve.wait_ge(s_zero, 3)
            for s in range(2):
                for h in range(2):
                    V.tensor_copy(vD[s][:, :, :, 32 + h],
                                  col["kv"][:, h:h + 1].unsqueeze(2).to_broadcast([P, 2, 8]))
            V.tensor_scalar(bq_quarter, bq_col, 0.25, None, ALU.mult)
            V.tensor_scalar(bo_rz, bo_bc, rz, None, ALU.mult).then_inc(s_hot, 1)
            dve.wait_ge(s_hot, 1)
            dve.wait_ge(s_sp1c, 1)

            def cT_add(i, odd):
                dve.wait_ge(cT_ps, i + 1)
                if not (isinstance(i, int) and i < 2):
                    dve.wait_ge(att_ps, i - 1)
                bias = cond_bT[:, ds(i * 2, 2), :].rearrange("p b m -> p m b").unsqueeze(3).to_broadcast(
                    [P, KC, 2, S])
                V.tensor_tensor(cT[int(odd)].rearrange("p m (b n) -> p m b n", b=2),
                                ps[:, 4, 0:D].rearrange("p (m b n) -> p m b n", m=KC, b=2), bias,
                                ALU.add).then_inc(cT_sb, 1)

            def k_spread(i):
                dve.wait_ge(k_ps, i + 1)
                for m in range(KC):
                    last = V.scalar_tensor_tensor(
                        out=kD[:, m], in0=ps[:, 4, m * P:(m + 1) * P].unsqueeze(1).to_broadcast([P, 2, P]),
                        scalar=bk_col[:, m:m + 1], in1=col["kmask"].unsqueeze(2).to_broadcast([P, 2, P]),
                        op0=ALU.add, op1=ALU.mult)
                last.then_inc(k_sb, 1)

            def v_spread(i, odd):
                dve.wait_ge(v_ps, i + 1)
                for h in range(2):
                    r = slice(h * S, (h + 1) * S)
                    last = V.tensor_tensor(
                        vD[int(odd)][r, :, :, h * HD:(h + 1) * HD],
                        ps[r, 6, 0:D].rearrange("p (b h d) -> p b h d", b=2, d=HD),
                        bv_half[r, :].rearrange("p (h d) -> p h d", d=HD).unsqueeze(1).to_broadcast([S, 2, 8, HD]),
                        ALU.add)
                last.then_inc(v_sb, 1)

            scores = ps[:, 0:4, 0:256].rearrange("p g (h k) -> p g h k", k=S)

            def shift(i):
                dve.wait_ge(s_ps, i + 1)
                V.tensor_reduce(smax.rearrange("p (g h) -> p g h", g=4), scores, AX.X, ALU.max).then_inc(max_sb, 1)
                dve.wait_ge(max_sb, i + 1)
                if not isinstance(i, int) or i > 0:
                    dve.wait_ge(pT_ps, 2 * i)
                V.tensor_tensor(probs.rearrange("p (g h k) -> p g h k", g=4, k=S), scores,
                                smax.rearrange("p (g h) -> p g h", g=4).unsqueeze(3).to_broadcast([P, 4, 4, S]),
                                ALU.subtract).then_inc(shift_sb, 1)

            def pT_copy(i):
                dve.wait_ge(pT_ps, 2 * i + 2)
                V.tensor_copy(probsT[:, 4:8, :].rearrange("p a n -> p (a n)"), ps[:, 1, :]).then_inc(pTv_sb, 1)

            o_acc = ps[:, 2, 0:8 * 34].rearrange("p (a n) -> p a n", n=34)

            def normalize(i):
                dve.wait_ge(o_ps, i + 1)
                V.reciprocal(rsum.rearrange("p (a h) -> p a h", h=2), o_acc[:, :, 32:34]).then_inc(rsum_sb, 1)
                dve.wait_ge(rsum_sb, i + 1)
                V.tensor_tensor(onorm.rearrange("p (a h d) -> p a h d", h=2, d=HD),
                                o_acc[:, :, 0:32].rearrange("p a (h d) -> p a h d", h=2),
                                rsum.rearrange("p (a h) -> p a h", h=2).unsqueeze(3).to_broadcast([P, 8, 2, HD]),
                                ALU.mult).then_inc(o_sb, 1)

            def x2_add(i, odd):
                s = int(odd)
                dve.wait_ge(att_ps, i + 1)
                dve.wait_ge(xbo_sb, i + 1)
                if not (isinstance(i, int) and i < 2):
                    dve.wait_ge(d_x2[s], turn(i, odd) - 16)
                V.tensor_tensor(x2[s], ps[:, 7, 0:D], x_bo[s], ALU.add).then_inc(x2_sb, 1)

            def t_mask(i):
                dve.wait_ge(t_ps, i + 1)
                if not isinstance(i, int) or i > 0:
                    dve.wait_ge(kept_t, i)
                hot = lang_hot[:, ds(i, 1), :].rearrange("p o l -> p (o l)")
                V.tensor_tensor(trow[:, 0:NLR].rearrange("p (l r) -> p l r", l=NLANG),
                                ps[:, 7, 0:NLR].rearrange("p (l r) -> p l r", l=NLANG),
                                hot.unsqueeze(2).to_broadcast([P, NLANG, RANK]), ALU.mult)
                V.tensor_copy(trow[:, NLR:NLR + NLANG], hot).then_inc(t_sb, 1)

            def logit_copy(i):
                dve.wait_ge(lg_ps, i + 1)
                V.tensor_scalar(logits[:, ds(i, 1), :].rearrange("p o n -> p (o n)"), ps[:, 7, 0:NE], 1.0 / TAU, None,
                                ALU.mult).then_inc(lg_sb, 1)

            def tile_steps(i, odd, first=False, last=False):
                if not last:
                    cT_add(i + 1, not odd)
                if not first:
                    x2_add(i - 1, not odd)
                shift(i)
                if not first:
                    t_mask(i - 1)
                if not last:
                    k_spread(i + 1)
                    v_spread(i + 1, not odd)
                pT_copy(i)
                if not first:
                    logit_copy(i - 1)
                normalize(i)

            cT_add(0, False)
            k_spread(0)
            v_spread(0, False)
            tile_steps(0, False, first=True)
            tile_steps(1, True)
            tile_steps(2, False)
            with dve.Fori(3, NT - 2, 2) as i:
                tile_steps(i, True)
                tile_steps(i + 1, False)
            tile_steps(NT - 1, True, last=True)
            x2_add(NT - 1, True)
            t_mask(NT - 1)
            logit_copy(NT - 1)

            dve.wait_ge(lg_sb, NT)
            down = col["count_down"].unsqueeze(1).to_broadcast([P, NT, NE])

            def over_e(x):
                return x.unsqueeze(2).to_broadcast([P, NT, NE])

            for cur, top, hot in ((logits[:, :, :], r_max1, r_m1), (r_a, r_max2, r_m2)):
                link(V.tensor_reduce(top, cur, AX.X, ALU.max))
                link(V.tensor_tensor(r_b, cur, over_e(top), ALU.is_equal))
                link(V.tensor_tensor(r_b, r_b, down, ALU.mult))
                link(V.tensor_reduce(r_s, r_b, AX.X, ALU.max))
                link(V.tensor_tensor(hot, r_b, over_e(r_s), ALU.is_equal))
                if hot is r_m1:
                    link(V.scalar_tensor_tensor(out=r_a, in0=r_m1, scalar=NEG, in1=logits[:, :, :],
                                                op0=ALU.mult, op1=ALU.add))
            V.tensor_tensor(chosen.rearrange("p (t e) -> p t e", e=NE), r_m1, r_m2, ALU.add).then_inc(r_chosen, 1)
            V.tensor_tensor(r_d, r_max2, r_max1, ALU.subtract).then_inc(r_gap, 1)
            dve.wait_ge(r_exp, 1)
            link(V.tensor_scalar(r_s, r_d, 1.0, None, ALU.add))
            link(V.reciprocal(gate[:, 0, :], r_s))
            link(V.tensor_tensor(gate[:, 1, :], gate[:, 0, :], r_d, ALU.mult))
            dve.wait_ge(r_rank, 1)
            link(V.tensor_reduce(r_n, ps[:, 1, 0:NT * NE].rearrange("p (t e) -> p e t", e=NE), AX.X, ALU.add))
            link(V.tensor_tensor(r_cmp, r_n.unsqueeze(2).to_broadcast([P, NE, NT]),
                                 col["tile_start"].unsqueeze(1).to_broadcast([P, NE, NT]), ALU.is_gt))
            link(V.tensor_reduce(r_tiles, r_cmp, AX.X, ALU.add))
            link(V.tensor_scalar(r_one, r_tiles, 0.0, 1.0, ALU.mult, ALU.add))
            link(V.tensor_tensor_scan(r_end, r_one, r_tiles, 0.0, ALU.mult, ALU.add))
            link(V.tensor_tensor(r_base, r_end, r_tiles, ALU.subtract))
            link(V.tensor_tensor(r_et, r_base.unsqueeze(1).to_broadcast([P, NS, NE]),
                                 col["slot_tile"].unsqueeze(2).to_broadcast([P, NS, NE]), ALU.is_le))
            link(V.tensor_reduce(r_ef, r_et, AX.X, ALU.add))
            link(V.tensor_scalar(expert_of[:, :], r_ef[0:1, :], -1.0, None, ALU.add))
            link(V.scalar_tensor_tensor(out=r_a, in0=r_base.unsqueeze(1).to_broadcast([P, NT, NE]),
                                        scalar=float(P), in1=ps[:, 0, 0:NT * NE].rearrange("p (t e) -> p t e", e=NE),
                                        op0=ALU.mult, op1=ALU.add))
            for k, hot in enumerate((r_m1, r_m2)):
                link(V.tensor_tensor(r_b, hot, r_a, ALU.mult))
                link(V.tensor_reduce(r_s, r_b, AX.X, ALU.add))
                ins = V.tensor_copy(slot[:, k, :], r_s)
                ins.then_inc(r_slots, 1)
            dve.wait_ge(r_slots, 2)
            V.tensor_copy(r_s, gate[:, 0, :]).then_inc(r_done, 1)

            def rowT_copy(t, s):
                dve.wait_ge(rowT_ps, t + 1)
                V.tensor_copy(s_rowT[s][0:TW, :], ps[0:TW, 7, 0:P]).then_inc(rowT_sb, 1)

            def multiply(n, j):
                dve.wait_ge(g_ok, n + 1)
                V.tensor_tensor(act_sb[j], ps[:, j, 0:CH], g_sb[j], ALU.mult).then_inc(act_ok, 1)

            def expert(eng, t):
                return eng.value_load(expert_of[0:1, ds(t, 1)], min_val=0, max_val=NE - 1)

            def routed_tiles(q, first=False, last=False):
                for s in range(3):
                    t = 3 * q + s
                    multiply(3 * t, 0)
                    if not (last and s == 2):
                        rowT_copy(t + 1, (s + 1) % 3)
                    multiply(3 * t + 1, 1)
                    if not (first and s == 0):
                        e = expert(dve, t - 1)
                        dve.wait_ge(y_ps, t)
                        if not (isinstance(q, int) and 3 * q + s - 1 < 3):
                            dve.wait_ge(d_y[(s - 1) % 3], 16 * (q - 1) if s == 0 else 16 * q)
                        V.tensor_tensor(y_sb[(s - 1) % 3], ps[:, 6, 0:D], be2_bc[:, ds(e * D, D)],
                                        ALU.add).then_inc(y_ok, 1)
                    multiply(3 * t + 2, 2)

            dve.wait_ge(d_be2, 16)
            rowT_copy(0, 0)
            routed_tiles(0, first=True)
            routed_tiles(1)
            with dve.Fori(2, NS // 3 - 1) as q:
                routed_tiles(q)
            routed_tiles(NS // 3 - 1, last=True)
            e = expert(dve, NS - 1)
            dve.wait_ge(y_ps, NS)
            dve.wait_ge(d_y[2], 16 * (NS // 3 - 1))
            V.tensor_tensor(y_sb[2], ps[:, 6, 0:D], be2_bc[:, ds(e * D, D)], ALU.add).then_inc(y_ok, 1)

            def sh_multiply(u, half):
                for c in range(4):
                    dve.wait_ge(shg_ok, 4 * u + (c + 1))
                    V.tensor_tensor(sh_aT[half][:, c, :], ps[:, 2 * (c % 2), :], sh_g[c % 2],
                                    ALU.mult).then_inc(sha_ok, 1)

            comb_base = [links[0]]

            def combine(u, v):
                n = 4 * u + v
                at0 = comb_base[0] + 3 * n
                dve.wait_ge(d_cx[v], 16 * u + 16)
                if not (isinstance(u, int) and u == 0):
                    dve.wait_ge(d_out[v], 16 * u)
                V.tensor_tensor(c_out[v], c_x2[v], bs2_bc[:, :], ALU.add).then_inc(chain, 1)
                dve.wait_ge(chain, at0 + 1)
                dve.wait_ge(shy_ps, n + 1)
                V.tensor_tensor(c_out[v], c_out[v], ps[:, 4 + v, 0:D], ALU.add).then_inc(chain, 1)
                dve.wait_ge(d_cy[v], 32 * u + 32)
                dve.wait_ge(chain, at0 + 2)
                V.scalar_tensor_tensor(out=c_out[v], in0=c_y[v][:, 0, :], scalar=gate[:, 0, ds(n, 1)],
                                       in1=c_out[v], op0=ALU.mult, op1=ALU.add).then_inc(chain, 1)
                dve.wait_ge(chain, at0 + 3)
                V.scalar_tensor_tensor(out=c_out[v], in0=c_y[v][:, 1, :], scalar=gate[:, 1, ds(n, 1)],
                                       in1=c_out[v], op0=ALU.mult, op1=ALU.add).then_inc(comb_ok, 1)

            def shared_two(w, last=False):
                sh_multiply(2 * w + 1, 1)
                for v in range(4):
                    combine(2 * w, v)
                if not last:
                    sh_multiply(2 * w + 2, 0)
                for v in range(4):
                    combine(2 * w + 1, v)

            sh_multiply(0, 0)
            shared_two(0)
            with dve.Fori(1, NT // 8 - 1) as w:
                shared_two(w)
            shared_two(NT // 8 - 1, last=True)

        @block.tensor
        def _(pe):
            mm, tr = nc.tensor.matmul, nc.tensor.transpose
            pe.wait_ge(d_setup, ALL_SETUP)
            pe.wait_ge(s_const, 3)
            for c in range(KC):
                tr(ps[:, 0, c * NLR:(c + 1) * NLR], lora_a[:, c * P:(c + 1) * P], ident[0:NLR, 0:NLR])
            for c in range(KC):
                mm(ps[0:NLR + NLANG, 0, 256:256 + NE], ba[:, c, :], wr_raw[:, c, :], start=(c == 0), stop=(c == KC - 1))
            for m in range(KC):
                last = mm(ps[:, 1, m * B:(m + 1) * B], cond_b[:, m * P:(m + 1) * P], cat_hot, start=True, stop=True)
            last.then_inc(s_sp1, 1)
            for n in range(4):
                for m in range(KC):
                    last = mm(ps[0:LR, 2 + n // 2, (n % 2) * D + m * P:(n % 2) * D + (m + 1) * P], b_raw[n][:, m, :],
                              ident, start=True, stop=True)
            last.then_inc(s_sp1, 1)
            pe.wait_ge(s_bT, 1)
            for n in range(4):
                for k in range(KC):
                    mm(ps[:, 4 + n, k * D:(k + 1) * D], a_raw[n][:, k * P:(k + 1) * P], bT[:, n, :],
                       start=True, stop=False)
                    for m in range(KC):
                        last = mm(ps[:, 4 + n, k * D + m * P:k * D + (m + 1) * P],
                                  w_raw[n][:, m, k * P:(k + 1) * P], ident, start=False, stop=(m == KC - 1))
                last.then_inc(s_mrg, 1)
            pe.wait_ge(s_mrgc, 4)
            pe.wait_ge(s_sp1c, 1)
            pe.wait_ge(s_zero, 4)

            def x_transpose(i, odd):
                s = int(odd)
                pe.wait_ge(d_x[s], turn(i, odd))
                if not isinstance(i, int) or i > 0:
                    pe.wait_ge(k_sb, i)
                for c in range(KC):
                    last = tr(ps[:, 4, c * P:(c + 1) * P], x_in[s][:, c * P:(c + 1) * P], ident)
                last.then_inc(xT_ps, 1)

            def condition(i, odd):
                s = int(odd)
                pe.wait_ge(d_cw[s], 2 * turn(i, odd))
                pe.wait_ge(xT_sb, i + 1)
                for m in range(KC):
                    for b in range(2):
                        for k in range(KC):
                            last = mm(ps[:, 4, m * P + b * S:m * P + (b + 1) * S],
                                      cond_w[s][:, b, k, m * P:(m + 1) * P], xT[:, k, b * S:(b + 1) * S],
                                      start=(k == 0), stop=(k == KC - 1))
                last.then_inc(cT_ps, 1)

            def project(i, odd):
                c = cT[int(odd)]
                pe.wait_ge(cT_sb, i + 1)
                if not isinstance(i, int) or i > 0:
                    pe.wait_ge(q_sb, i)
                    pe.wait_ge(v_sb, i)
                for w, bank, done in ((1, 4, k_ps), (0, 5, q_ps)):
                    for m in range(KC):
                        for k in range(KC):
                            last = mm(ps[:, bank, m * P:(m + 1) * P], wm[w][:, k, m * P:(m + 1) * P], c[:, k, :],
                                      start=(k == 0), stop=(k == KC - 1))
                    last.then_inc(done, 1)
                wv = [wm[2][:, k, :].rearrange("p (h two d) -> p two h d", two=2, d=HD) for k in range(KC)]
                for b in range(2):
                    for h in range(2):
                        for k in range(KC):
                            last = mm(ps[h * S:(h + 1) * S, 6, b * P:(b + 1) * P].rearrange("p (h d) -> p h d", d=HD),
                                      c[:, k, b * S:(b + 1) * S], wv[k][:, h], start=(k == 0), stop=(k == KC - 1))
                last.then_inc(v_ps, 1)

            def score(i):
                pe.wait_ge(q_sb, i + 1)
                pe.wait_ge(k_sb, i + 1)
                if not isinstance(i, int) or i > 0:
                    pe.wait_ge(pTa_sb, i)
                    pe.wait_ge(pTv_sb, i)
                    pe.wait_ge(o_sb, i)
                for g in range(4):
                    mm(ps[:, g, 0:256], ali[:, 0:P], ali[:, P + g * 256:P + (g + 1) * 256], start=True, stop=False)
                for m in range(KC):
                    for b in range(2):
                        for g in range(4):
                            r = slice(32 * g, 32 * g + 32)
                            last = mm(ps[b * S:(b + 1) * S, g, m * P:(m + 1) * P].rearrange("p (h k) -> p h k", h=2),
                                      qT[r, m, b * S:(b + 1) * S], kD[r, m, :, b * S:(b + 1) * S],
                                      start=False, stop=(m == KC - 1))
                last.then_inc(s_ps, 1)

            def prob_transpose(i):
                pe.wait_ge(prob_sb, i + 1)
                for n in range(8):
                    last = tr(ps[:, n // 4, (n % 4) * P:(n % 4 + 1) * P], probs[:, n * P:(n + 1) * P], ident)
                    if n % 4 == 3:
                        last.then_inc(pT_ps, 1)

            def attend(i, odd):
                pe.wait_ge(pTa_sb, i + 1)
                pe.wait_ge(pTv_sb, i + 1)
                pe.wait_ge(v_sb, i + 1)
                for g in range(4):
                    for m in range(KC):
                        hp = 4 * m + g
                        for b in range(2):
                            last = mm(ps[b * S:(b + 1) * S, 2, hp * 34:(hp + 1) * 34],
                                      probsT[:, 2 * g + m, b * S:(b + 1) * S], vD[int(odd)][:, b, hp, :],
                                      start=True, stop=True)
                last.then_inc(o_ps, 1)

            def o_transpose(i):
                pe.wait_ge(o_sb, i + 1)
                if not isinstance(i, int) or i > 0:
                    pe.wait_ge(lg_sb, i)
                for c in range(KC):
                    last = tr(ps[:, 7, c * P:(c + 1) * P], onorm[:, c * P:(c + 1) * P], ident)
                last.then_inc(oT_ps, 1)

            def output(i, odd):
                pe.wait_ge(oT_sb, i + 1)
                for k in range(KC):
                    mm(ps[:, 7, 0:D], oT[:, k, :], wm[3][:, k, :], start=(k == 0), stop=False)
                for k in range(KC):
                    last = mm(ps[:, 7, k * P:(k + 1) * P], cT[int(odd)][:, k, :], ident, start=False,
                              stop=(k == KC - 1))
                last.then_inc(att_ps, 1)

            def x2_transpose(i, odd):
                pe.wait_ge(x2_sb, i + 1)
                for c in range(KC):
                    last = tr(ps[:, 7, c * P:(c + 1) * P], x2[int(odd)][:, c * P:(c + 1) * P], ident)
                last.then_inc(x2T_ps, 1)

            def low_rank(i):
                pe.wait_ge(x2T_sb, i + 1)
                for c in range(KC):
                    last = mm(ps[:, 7, 0:NLR], x2T[:, c, :], aT[:, c, :], start=(c == 0), stop=(c == KC - 1))
                last.then_inc(t_ps, 1)

            def row_transpose(i):
                pe.wait_ge(t_sb, i + 1)
                tr(ps[0:TW, 7, 0:P], trow[:, 0:TW], ident).then_inc(tT_ps, 1)

            def router(i):
                pe.wait_ge(tT_sb, i + 1)
                mm(ps[:, 7, 0:NE], trowT[0:TW, :], wr[0:TW, :], start=True, stop=True).then_inc(lg_ps, 1)

            def tile_steps(i, odd, first=False, last=False):
                if not last:
                    x_transpose(i + 1, not odd)
                if not first:
                    o_transpose(i - 1)
                if not last:
                    condition(i + 1, not odd)
                if not first:
                    output(i - 1, not odd)
                score(i)
                if not first:
                    x2_transpose(i - 1, not odd)
                if not last:
                    project(i + 1, not odd)
                if not first:
                    low_rank(i - 1)
                    row_transpose(i - 1)
                prob_transpose(i)
                if not first:
                    router(i - 1)
                attend(i, odd)

            x_transpose(0, False)
            condition(0, False)
            project(0, False)
            tile_steps(0, False, first=True)
            tile_steps(1, True)
            tile_steps(2, False)
            with pe.Fori(3, NT - 2, 2) as i:
                tile_steps(i, True)
                tile_steps(i + 1, False)
            tile_steps(NT - 1, True, last=True)
            o_transpose(NT - 1)
            output(NT - 1, True)
            x2_transpose(NT - 1, True)
            low_rank(NT - 1)
            row_transpose(NT - 1)
            router(NT - 1)

            def merge(j, arrived, n, filled=True):
                pe.wait_ge(d_stage[j], arrived)
                if filled:
                    pe.wait_ge(merge_sb, n - 2)
                for c in range(KC):
                    last = mm(ps[0:NLR + NLANG, 3 + j, :], ba[:, c, :], stage_w[j][:, c, :],
                              start=(c == 0), stop=(c == KC - 1))
                last.then_inc(merge_ps, 1)

            for j in range(NJ):
                merge(j, 32, j, filled=False)
            pe.wait_ge(r_chosen, 1)
            n = NT * NE
            mm(ps[:, 0, 0:n], tri_b[:, :], chosen, start=True, stop=False)
            for back in range(1, NT):
                mm(ps[:, 0, back * NE:n], ones_b[:, :], chosen[:, 0:n - back * NE], start=False,
                   stop=(back == NT - 1))
            mm(ps[:, 1, 0:n], ones_b[:, :], chosen, start=True, stop=True).then_inc(r_rank, 1)
            with pe.Fori(1, NE) as e:
                for j in range(NJ):
                    merge(j, 32 * e + 32, 3 * e + j)
            for j in range(HS // CH):
                merge(j, 32 * (NE + 1), NE * NJ + j)

            def rows_transpose(t, s, arrived):
                pe.wait_ge(d_row[s], arrived)
                if not isinstance(t, int) or t > 0:
                    pe.wait_ge(rowT_sb, t)
                tr(ps[0:TW, 7, 0:P], s_row[s][:, 0:TW], ident).then_inc(rowT_ps, 1)

            def first_layer(t, s, j, e):
                if j == 0:
                    pe.wait_ge(rowT_sb, t + 1)
                mm(ps[:, j, :], s_rowT[s][0:TW, :], w1m[0:TW, w1_cols(e, j)], start=True, stop=True).then_inc(h_ps, 1)

            def act_transpose(n, j):
                pe.wait_ge(act_ok, n + 1)
                for c in range(2):
                    last = tr(ps[:, 3 + j, c * P:(c + 1) * P], act_sb[j][:, c * P:(c + 1) * P], ident)
                last.then_inc(actT_ps, 1)

            def second_layer(t, j, e):
                pe.wait_ge(actT_ok, 3 * t + (j + 1))
                if j == 0 and (not isinstance(t, int) or t > 0):
                    pe.wait_ge(y_ok, t)
                for c in range(2):
                    last = mm(ps[:, 6, 0:D], actT_sb[j][:, c, :], arena[:, ds(e * E2 + (2 * j + c) * D, D)],
                              start=(j == 0 and c == 0), stop=(j == NJ - 1 and c == 1))
                if j == NJ - 1:
                    last.then_inc(y_ps, 1)

            def expert(t):
                return pe.value_load(expert_of[0:1, ds(t, 1)], min_val=0, max_val=NE - 1)

            def routed_tiles(q, first=False, last=False):
                ex = {s: expert(3 * q + s) for s in range(-1, 4) if not (first and s < 0) and not (last and s > 2)}
                for s in range(3):
                    t = 3 * q + s
                    more = not (last and s == 2)
                    if more:
                        rows_transpose(t + 1, (s + 1) % 3, 16 * q + (32 if s == 2 else 16))
                    first_layer(t, s, 2, ex[s])
                    act_transpose(3 * t, 0)
                    if not (first and s == 0):
                        second_layer(t - 1, 2, ex[s - 1])
                    for j in (1, 2):
                        if more:
                            first_layer(t + 1, (s + 1) % 3, j - 1, ex[s + 1])
                        act_transpose(3 * t + j, j)
                        second_layer(t, j - 1, ex[s])

            pe.wait_ge(d_w1bias, 16 * len(be1_rows))
            pe.wait_ge(merge_sb, n_merge)
            pe.wait_ge(d_w2, 16 * (NE + 1))
            rows_transpose(0, 0, 16)
            e0 = expert(0)
            first_layer(0, 0, 0, e0)
            first_layer(0, 0, 1, e0)
            routed_tiles(0, first=True)
            routed_tiles(1)
            with pe.Fori(2, NS // 3 - 1) as q:
                routed_tiles(q)
            routed_tiles(NS // 3 - 1, last=True)
            second_layer(NS - 1, 2, expert(NS - 1))

            def hidden(u):
                for c in range(4):
                    for g in range(2):
                        at_col = NE * EW + (c // 2) * 2 * CH + g * CH + (c % 2) * P
                        if g == 0 and not (isinstance(u, int) and u == 0 and c < 2):
                            pe.wait_ge(sha_ok, 4 * u + (c - 1))
                        last = mm(ps[:, 2 * (c % 2) + g, :], w1m[0:TW, at_col:at_col + P],
                                  ltT[0:TW, ds(u * 512, 512)], start=True, stop=True)
                    last.then_inc(sh_ps, 1)

            def shared_out(u, half):
                pe.wait_ge(sha_ok, 4 * u + 4)
                for v in range(4):
                    if not (isinstance(u, int) and u == 0):
                        pe.wait_ge(comb_ok, 4 * u + (v - 3))
                    for k in range(HS // P):
                        last = mm(ps[:, 4 + v, 0:D], sh_aT[half][:, k, v * P:(v + 1) * P], ws2[:, k, :],
                                  start=(k == 0), stop=(k == HS // P - 1))
                    last.then_inc(shy_ps, 1)

            pe.wait_ge(y_ok, NS)
            def shared_two(w):
                hidden(2 * w + 1)
                shared_out(2 * w, 0)
                hidden(2 * w + 2)
                shared_out(2 * w + 1, 1)

            hidden(0)
            shared_two(0)
            with pe.Fori(1, NT // 8 - 1) as w:
                shared_two(w)
            hidden(NT // 4 - 1)
            shared_out(NT // 4 - 2, 0)
            shared_out(NT // 4 - 1, 1)


def shape_constants():
    c = np.zeros((P, sum(CONST_COLS.values())), np.float32)
    at, p = 0, np.arange(P)
    cols = {
        "ident": np.eye(P), "tri": (p[:, None] < p[None, :]),
        "kmask": ((p[:, None] % 32) // HD == np.arange(2)[None, :]),
        "kv": (p[:, None] // S == np.arange(2)[None, :]),
        "count_down": np.broadcast_to(NE - np.arange(NE), (P, NE)),
        "tile_start": np.broadcast_to(P * np.arange(NT), (P, NT)),
        "slot_tile": np.broadcast_to(np.arange(NS), (P, NS)), "part": p[:, None],
    }
    for name, n in CONST_COLS.items():
        c[:, at:at + n] = cols[name]
        at += n
    ali = np.zeros((2, P + H * S), np.float32)
    ali[0, :P] = 1.0
    ali[1, :P] = p % S
    slopes = np.array([0.5 ** (m * 8 + g * 2 + h) for g in range(4) for m in range(2) for h in range(2)])
    ali[0, P:] = (slopes[:, None] * np.arange(S)[None, :]).reshape(-1)
    ali[1, P:] = np.repeat(-slopes, S)
    return c, ali


_INS = ['x', 'itok_B_0_15', 'itok_B_0_3', 'L0_cond_weight', 'L0_cond_bias', 'L0_attn_Wq', 'L0_attn_bq', 'L0_attn_Aq',
        'L0_attn_Bq', 'L0_attn_Wk', 'L0_attn_bk', 'L0_attn_Ak', 'L0_attn_Bk', 'L0_attn_Wv', 'L0_attn_bv',
        'L0_attn_Av', 'L0_attn_Bv', 'L0_attn_Wo', 'L0_attn_bo', 'L0_attn_Ao', 'L0_attn_Bo', 'L0_attn_rezero',
        'L0_cond2_lora_A', 'L0_cond2_lora_B', 'L0_cond2_lang_embed', 'L0_ffn_Ws1', 'L0_ffn_bs1', 'L0_ffn_Ws2',
        'L0_ffn_bs2', 'L0_ffn_We1', 'L0_ffn_be1', 'L0_ffn_We2', 'L0_ffn_be2', 'L0_ffn_Wr', 'L0_ffn_br']


def kernel(**inputs):
    import concourse.bacc as bacc
    from concourse.bass_utils import run_bass_kernel_spmd

    nc = bacc.Bacc("TRN2", target_bir_lowering=False, num_devices=1)
    consts, alibi = shape_constants()
    given = {name: np.ascontiguousarray(inputs[name]) for name in _INS}
    given["consts"], given["alibi"] = consts, alibi
    arrays, args = {}, {}
    for name, arr in given.items():
        arrays[f"in_{name}_dram"] = arr
        args[name] = nc.dram_tensor(f"in_{name}_dram", arr.shape, mybir.dt.from_np(arr.dtype),
                                    kind="ExternalInput").ap()
    out = nc.dram_tensor("out_0_dram", (B, S, D), mybir.dt.float32, kind="ExternalOutput").ap()
    adaln_attn_moe(nc, args, out)
    r = run_bass_kernel_spmd(nc, [arrays], core_ids=[0])
    return r.results[0]["out_0_dram"]
```

```python
import numpy as np
import concourse.bass as bass
from concourse import mybir
from contextlib import ExitStack

P = 128
B, S, D = 64, 64, 256
H, HD = 16, 16
NCAT, NLANG, RANK, LR = 16, 4, 16, 8
NE, HR, HS = 12, 768, 512
TAU = 1.5
TOK = B * S
NT = TOK // P
KC = D // P
U = 2 * P
NLR = NLANG * RANK
TW = NLR + NLANG + 1
TWP = 72
W_COL, ID_COL = TW, TW + 1
NS = (2 * TOK + NE * (P - 1)) // P
CH = 256
NJ = HR // CH
EW = 2 * HR
E2 = HR // P * D
RING = 6
YR = 3
NEG = -3.0e38
CONST_COLS = dict(ident=P, tri=P, kmask=2, kv=2, count_down=NE, tile_start=NT, slot_tile=NS)


def adaln_attn_moe(nc, args, out):
    f32, bf16, i32, u32 = mybir.dt.float32, mybir.dt.bfloat16, mybir.dt.int32, mybir.dt.uint32
    ALU, ACT, AX = mybir.AluOpType, mybir.ActivationFunctionType, mybir.AxisListType
    ds = bass.ds
    a = args
    x_rows = a["x"].rearrange("b s d -> (b s) d")
    out_rows = out
    cond_w_dram = a["L0_cond_weight"].rearrange("k (c p) n -> k p c n", p=P)

    ctx = ExitStack()
    with ctx:
        def sb(name, shape, dt=f32):
            return ctx.enter_context(nc.sbuf_tensor(name, shape, dt))

        def sem(name):
            return ctx.enter_context(nc.semaphore(name))

        x2_dram = nc.dram_tensor("x2_dram", [TOK, D], f32).ap()
        slot_rows = nc.dram_tensor("slot_rows", [NS * P, TWP], f32).ap()

        consts = sb("consts", [P, sum(CONST_COLS.values())])
        col, at = {}, 0
        for name, n in CONST_COLS.items():
            col[name] = consts[:, at:at + n]
            at += n
        ident = col["ident"]
        w1m = sb("w1_merged", [P, NE * EW + 2 * HS])
        lrows = sb("token_rows", [P, NT, TWP])
        ltT = sb("token_rows_T", [P, TOK])
        logits = sb("logits", [P, NT, NE])
        gate = sb("gate", [P, 2, NT])
        slot = sb("slot", [P, 2, NT], u32)
        expert_of = sb("expert_of", [1, NS], i32)
        be2_bc = sb("be2_bc", [P, NE * D])
        stage = sb("stage", [P, NJ * 1024])
        bs2_bc = sb("bs2_bc", [P, D])
        arena = sb("arena", [P, NE * E2 + HS // P * D])

        class Cut:
            def __init__(self, tensor):
                self.tensor, self.at = tensor, 0
                self.flat = tensor[:, :] if len(tensor.shape) == 2 else tensor[:, :, :].rearrange("p a b -> p (a b)")

            def __call__(self, *shape, parts=P):
                n = 1
                for s in shape:
                    n *= s
                ap = self.flat[0:parts, self.at:self.at + n]
                self.at += n
                assert self.at <= self.flat.shape[1]
                if len(shape) == 1:
                    return ap
                names = "abcde"[:len(shape)]
                dims = {k: v for k, v in zip(names, shape)}
                return ap.rearrange(f"p ({' '.join(names)}) -> p {' '.join(names)}", **dims)

        cut = Cut(arena)
        x_in = [cut(D) for _ in range(2)]
        x_res = [cut(D) for _ in range(2)]
        cond_bias = [cut(D) for _ in range(2)]
        c_sb = cut(D)
        cond_w = [cut(2, KC, D) for _ in range(2)]
        xT = cut(KC, P)
        cT = cut(KC, P)
        qT = cut(KC, P)
        kD = cut(KC, 2, P)
        vD = [cut(2, 8, 34) for _ in range(2)]
        probs = cut(1024)
        probsT = cut(8, P)
        onorm = cut(D)
        oT = cut(KC, P)
        x2 = [cut(D) for _ in range(2)]
        x2T = cut(KC, P)
        trow = cut(TWP)
        trowT = cut(P)
        smax = cut(H)
        rsum = cut(H)
        wm = [cut(KC, D) for _ in range(4)]
        w_raw = [cut(KC, D) for _ in range(4)]
        a_raw = [cut(D, parts=LR) for _ in range(4)]
        b_raw = [cut(KC, LR) for _ in range(4)]
        bT = cut(4, D, parts=LR)
        lora_a = cut(D, parts=NLR)
        aT = cut(KC, NLR)
        bq_col, bk_col, bq_quarter, rz = cut(KC), cut(KC), cut(KC), cut(1)
        bv_half = cut(P)
        bo_bc, bo_rz = cut(D), cut(D)
        wr_raw = cut(KC, NE)
        wr = cut(NE)
        lang_f = cut(NT)
        lang_hot = cut(NT, NLANG)
        ali_f = cut(P + H * S, parts=2)
        ali = cut((P + H * S) // 2, parts=2).bitcast(bf16)
        ba = sb("ba", [P, KC, NLR + NLANG])
        cat_i = sb("cat_i", [1, B], i32)
        lang_i = sb("lang_i", [P, NT], i32)
        tok_id = sb("tok_id", [P, NT + 1], i32)
        tri_b = sb("tri_b", [P, P], bf16)
        ones_b = sb("ones_b", [P, P], bf16)
        cut = Cut(be2_bc)
        r_a, r_b, r_m1, r_m2 = [cut(NT, NE) for _ in range(4)]
        r_max1, r_max2, r_s, r_d = [cut(NT) for _ in range(4)]
        r_n, r_tiles, r_end, r_base, r_one = [cut(NE) for _ in range(5)]
        r_et = cut(NS, NE)
        r_cmp = r_et.rearrange("p t e -> p (t e)")[:, 0:NE * NT].rearrange("p (e t) -> p e t", e=NE)
        r_ef = cut(NS)
        chosen = cut(NT * NE // 2).bitcast(bf16)
        stage_w = [stage[:, j * 1024:(j + 1) * 1024].rearrange("p (c n) -> p c n", c=KC) for j in range(NJ)]
        cut = Cut(stage)
        g_sb = [cut(CH) for _ in range(NJ)]
        actT_sb = [cut(2, P) for _ in range(NJ)]
        y_sb = [cut(D) for _ in range(YR)]
        cut = Cut(lrows)
        s_row = [cut(TWP) for _ in range(RING)]
        s_rowT = [cut(P) for _ in range(2)]
        cut = Cut(ltT)
        w1x = [cut(EW, parts=TW) for _ in range(2)]
        gated_be2 = [cut(D) for _ in range(2)]
        cut = Cut(stage)
        sh_g = [cut(U) for _ in range(2)]
        sh_aT = [cut(HS // P, U) for _ in range(2)]
        c_x2 = [cut(D) for _ in range(2)]
        ws2 = arena[:, NE * E2:].rearrange("p (k n) -> p k n", n=D)

        ps = ctx.enter_context(nc.psum_tensor("ps", [P, 8, 512], f32))

        d_setup, d_w1bias, d_zero = sem("d_setup"), sem("d_w1bias"), sem("d_zero")
        d_x = [sem(f"d_x{s}") for s in range(2)]
        d_cw = [sem(f"d_cw{s}") for s in range(2)]
        d_cb = [sem(f"d_cb{s}") for s in range(2)]
        d_x2 = [sem(f"d_x2{s}") for s in range(2)]
        s_const, s_hot, s_sp1, s_sp1c, s_bT, s_mrg, s_mrgc = [sem(n) for n in (
            "s_const", "s_hot", "s_sp1", "s_sp1c", "s_bT", "s_mrg", "s_mrgc")]
        s_zero, s_id = sem("s_zero"), sem("s_id")
        chain = sem("chain")
        (xT_ps, xT_sb, c_ps, c_ok, cT_ps, cT_sb, xbo_sb, xres_sb, q_ps, q_sb, kv_ps, k_sb, v_sb, s_ps, max_sb, shift_sb,
         prob_sb, pT_ps, pTa_sb, pTv_sb, o_ps, rsum_sb, o_sb, oT_ps, oT_sb, att_ps, x2_sb, x2T_ps, x2T_sb,
         t_ps, t_sb, tT_ps, tT_sb, lg_ps, lg_sb, kept_t, kept_tT) = [sem(n) for n in (
             "xT_ps xT_sb c_ps c_ok cT_ps cT_sb xbo_sb xres_sb q_ps q_sb kv_ps k_sb v_sb s_ps max_sb shift_sb "
             "prob_sb pT_ps pTa_sb pTv_sb o_ps rsum_sb o_sb oT_ps oT_sb att_ps x2_sb x2T_ps x2T_sb "
             "t_ps t_sb tT_ps tT_sb lg_ps lg_sb kept_t kept_tT").split()]
        d_stage = [sem(f"d_stage{j}") for j in range(NJ)]
        d_w2, d_be2, d_scatter, gate_col = sem("d_w2"), sem("d_be2"), sem("d_scatter"), sem("gate_col")
        merge_ps, merge_sb, r_gap, r_exp, r_chosen, r_rank, r_slots, r_gates, r_done = [sem(n) for n in (
            "merge_ps", "merge_sb", "r_gap", "r_exp", "r_chosen", "r_rank", "r_slots", "r_gates", "r_done")]
        d_row = [sem(f"d_row{s}") for s in range(RING)]
        d_add = sem("d_add")
        w1x_ok = [sem(f"w1x_ok{j}") for j in range(NJ)]
        (rowT_ps, rowT_sb, h_ps, g_ok, act_ok, gb_ok, y_ps, y_ok) = [sem(n) for n in (
            "rowT_ps", "rowT_sb", "h_ps", "g_ok", "act_ok", "gb_ok", "y_ps", "y_ok")]
        d_cx = [sem(f"d_cx{s}") for s in range(2)]
        d_out = [sem(f"d_out{s}") for s in range(2)]
        d_dummy, d_ws2 = sem("d_dummy"), sem("d_ws2")
        sh_ps, shg_ok, sha_ok, shy_ps, bs2_ok, comb_ok = [sem(n) for n in (
            "sh_ps", "shg_ok", "sha_ok", "shy_ps", "bs2_ok", "comb_ok")]

        names = "qkvo"
        loads = [(consts[:, :], a["consts"]), (ali_f, a["alibi"])]
        for n, c in enumerate(names):
            loads += [(w_raw[n], a[f"L0_attn_W{c}"].rearrange("(m p) n -> p m n", p=P)),
                      (a_raw[n], a[f"L0_attn_A{c}"]),
                      (b_raw[n], a[f"L0_attn_B{c}"].rearrange("(m p) n -> p m n", p=P))]
        loads += [
            (lora_a, a["L0_cond2_lora_A"].rearrange("l r d -> (l r) d")),
            (cat_i[:, :], a["itok_B_0_15"].unsqueeze(0)),
            (bq_col, a["L0_attn_bq"].rearrange("(m p) -> p m", p=P)),
            (bk_col, a["L0_attn_bk"].rearrange("(m p) -> p m", p=P)),
            (rz, a["L0_attn_rezero"].partition_broadcast(P)),
            (bo_bc, a["L0_attn_bo"].partition_broadcast(P)),
            (bs2_bc[:, :], a["L0_ffn_bs2"].partition_broadcast(P)),
            (wr_raw, a["L0_ffn_Wr"].rearrange("(c p) n -> p c n", p=P)),
            (wr[TW - 1:TW, :], a["L0_ffn_br"].unsqueeze(0)),
        ]
        for c in range(KC):
            loads.append((ba[:, c, NLR:NLR + NLANG],
                          a["L0_cond2_lang_embed"][:, c * P:(c + 1) * P].rearrange("l p -> p l")))
            for lang in range(NLANG):
                loads.append((ba[:, c, lang * RANK:(lang + 1) * RANK],
                              a["L0_cond2_lora_B"][lang, c * P:(c + 1) * P, :]))
        for h in range(2):
            loads.append((bv_half[h * S:(h + 1) * S, :].rearrange("p (h d) -> p h d", d=HD),
                          a["L0_attn_bv"].rearrange("(h two d) -> two h d", two=2, d=HD)[h].partition_broadcast(S)))
            loads.append((lang_i[h * S:(h + 1) * S, :],
                          a["itok_B_0_3"].rearrange("(t two) -> two t", two=2)[h].partition_broadcast(S)))
        ALL_SETUP = 16 * len(loads)
        be1_rows = [(w1m[TW - 1:TW, 0:NE * EW].rearrange("p (e j g n) -> p g e j n", e=NE, j=NJ, g=2)[:, g],
                     a["L0_ffn_be1"][:, g * HR:(g + 1) * HR].rearrange("e (j n) -> e j n", j=NJ).unsqueeze(0))
                    for g in range(2)]
        be1_rows += [(w1m[TW - 1:TW, NE * EW:].rearrange("p (j g n) -> p g j n", j=HS // CH, g=2)[:, g],
                      a["L0_ffn_bs1"][g * HS:(g + 1) * HS].rearrange("(j n) -> j n", n=CH).unsqueeze(0))
                     for g in range(2)]

        def turn(i, odd):
            return 8 * i + (8 if odd else 16)

        def w1_cols(e, j):
            return ds(e * EW + j * 2 * CH, 2 * CH)

        def copy_first(engine, copy, t, s, j):
            e = engine.value_load(expert_of[0:1, ds(t, 1)], min_val=0, max_val=NE - 1)
            copy(w1x[s % 2][:, j * 2 * CH:(j + 1) * 2 * CH], w1m[0:TW, w1_cols(e, j)]).then_inc(w1x_ok[j], 1)

        n_merge = NE * NJ + HS // CH

        block = ctx.enter_context(nc.Block())

        @block.sync
        def _(sp):
            for dst, src in loads[0::2]:
                with nc.allow_non_contiguous_dma(reason="a few hundred words of biases, embeddings and ids"):
                    sp.dma_start(dst, src).then_inc(d_setup, 16)

            def load_first(j, src):
                for c in range(KC):
                    sp.dma_start(stage_w[j][:, c, :].rearrange("p (g n) -> p g n", g=2),
                                 src[c * P:(c + 1) * P].rearrange("p (g n) -> p g n", g=2)[
                                     :, :, j * CH:(j + 1) * CH]).then_inc(d_stage[j], 16)

            def first_of(e):
                return a["L0_ffn_We1"][ds(e, 1), :, :].rearrange("o d n -> (o d) n")

            for j in range(HS // CH):
                load_first(j, a["L0_ffn_Ws1"])
            for dst, src in be1_rows:
                sp.dma_start(dst, src).then_inc(d_w1bias, 16)
            sp.wait_ge(d_setup, ALL_SETUP)

            def load_tile(i, odd):
                s = int(odd)
                if not (isinstance(i, int) and i < 2):
                    sp.wait_ge(xbo_sb, i - 1)
                    sp.wait_ge(c_ok, i - 1)
                sp.dma_start(x_in[s], x_rows[ds(i * P, P), :]).then_inc(d_x[s], 16)
                for b in range(2):
                    cat = sp.value_load(cat_i[0:1, ds(i * 2 + b, 1)], min_val=0, max_val=NCAT - 1)
                    sp.dma_start(cond_w[s][:, b], cond_w_dram[ds(cat, 1), :, :, :].rearrange(
                        "o p c n -> p (o c) n")).then_inc(d_cw[s], 16)
                    sp.dma_start(cond_bias[s][b * S:(b + 1) * S, :], a["L0_cond_bias"][ds(cat, 1), :].rearrange(
                        "o n -> (o n)").partition_broadcast(S)).then_inc(d_cb[s], 16)

            def store_x2(i, odd):
                sp.wait_ge(x2_sb, i + 1)
                sp.dma_start(x2_dram[ds(i * P, P), :], x2[int(odd)]).then_inc(d_x2[int(odd)], 16)

            load_tile(0, False)
            load_tile(1, True)
            load_tile(2, False)
            load_first(2, first_of(0))
            load_tile(3, True)
            for i in range(1, 3):
                store_x2(i - 1, i == 2)
                load_tile(i + 3, i == 2)
                sp.wait_ge(merge_ps, i)
                load_first(i - 1, first_of(0))

            def two_steps(e, more):
                i = 2 * e + 3
                store_x2(i - 1, False)
                load_tile(i + 3, False)
                if more:
                    for j in (0, 1):
                        sp.wait_ge(merge_ps, 3 * e + (j + 3))
                        load_first(j, first_of(e + 1))
                store_x2(i, True)
                load_tile(i + 4, True)
                if more:
                    sp.wait_ge(merge_ps, 3 * e + 5)
                    load_first(2, first_of(e + 1))

            with sp.Fori(0, NE - 1) as e:
                two_steps(e, True)
            two_steps(NE - 1, False)
            for i in range(2 * NE + 3, NT + 1):
                store_x2(i - 1, i % 2 == 0)
                if i + 3 < NT:
                    load_tile(i + 3, i % 2 == 0)

            sp.wait_ge(lg_sb, NT)
            sp.wait_ge(kept_t, NT)
            sp.wait_ge(kept_tT, NT)
            for s in range(2):
                sp.wait_ge(d_x2[s], 16 * NT // 2)
            sp.dma_start(ws2, a["L0_ffn_Ws2"].rearrange("(k p) n -> p k n", p=P)).then_inc(d_ws2, 16)

            def load_x2(n, v):
                sp.dma_start(c_x2[v], x2_dram[ds(n * P, P), :]).then_inc(d_cx[v], 16)

            def store_out(n, v):
                sp.wait_ge(comb_ok, n + 1)
                sp.dma_start(out_rows[ds(n * P, P), :], c_x2[v]).then_inc(d_out[v], 16)

            def load_second(e):
                src = a["L0_ffn_We2"][ds(e, 1), :, :].rearrange("o (k p) n -> p (o k) n", p=P)
                sp.dma_start(arena[:, ds(e * E2, E2)].rearrange("p (k n) -> p k n", n=D), src).then_inc(d_w2, 16)

            sp.wait_ge(merge_ps, n_merge)
            for v in range(2):
                load_x2(v, v)
            with sp.Fori(0, NE) as e:
                for v in range(2):
                    store_out(2 * e + v, v)
                load_second(e)
                for v in range(2):
                    sp.wait_ge(d_out[v], 16 * e + 16)
                    load_x2(2 * e + (v + 2), v)
            for u in range(NE, NT // 2):
                for v in range(2):
                    store_out(2 * u + v, v)
                if u < NT // 2 - 1:
                    for v in range(2):
                        sp.wait_ge(d_out[v], 16 * u + 16)
                        load_x2(2 * u + 2 + v, v)
                if u == NT // 2 - 3:
                    sp.wait_ge(r_done, 1)
                    sp.dma_start(be2_bc[:, :], a["L0_ffn_be2"].rearrange("e n -> (e n)").partition_broadcast(P)
                                 ).then_inc(d_be2, 16)

            def load_rows(t, s):
                if not (isinstance(t, int) and t < RING):
                    sp.wait_ge(d_add, 16 * t - 16 * (RING - 1))
                sp.dma_start(s_row[s], slot_rows[ds(t * P, P), :]).then_inc(d_row[s], 16)

            sp.wait_ge(d_scatter, 16 * 2 * NT)
            for s in range(RING):
                load_rows(s, s)
            with sp.Fori(1, NS // RING) as q:
                for s in range(RING):
                    load_rows(RING * q + s, s)
            for s in range(NS % RING):
                load_rows(NS - NS % RING + s, s)

        @block.gpsimd
        def _(pool):
            zeros = lrows[:, 0, :]
            nc.gpsimd.memset(lrows[:, :, :], 0.0).then_inc(s_zero, 1)
            for s in range(2):
                nc.gpsimd.memset(vD[s], 0.0).then_inc(s_zero, 1)
            nc.gpsimd.memset(ones_b[:, :], 1.0).then_inc(s_zero, 1)
            nc.gpsimd.memset(trow, 1.0).then_inc(s_zero, 1)
            def residual(i, odd):
                s = int(odd)
                pool.wait_ge(d_x[s], turn(i, odd))
                if not (isinstance(i, int) and i < 2):
                    pool.wait_ge(x2_sb, i - 1)
                nc.gpsimd.tensor_tensor(x_res[s], x_in[s], bo_rz, ALU.add).then_inc(xbo_sb, 1)

            def residual_c(i, odd):
                s = int(odd)
                pool.wait_ge(c_ok, i + 1)
                pool.wait_ge(xbo_sb, i + 1)
                nc.gpsimd.tensor_tensor(x_res[s], x_res[s], c_sb, ALU.add).then_inc(xres_sb, 1)

            def keep(i):
                pool.wait_ge(t_sb, i + 1)
                nc.gpsimd.tensor_copy(lrows[:, ds(i, 1), 0:NLR].rearrange("p o n -> p (o n)"),
                                      trow[:, 0:NLR]).then_inc(kept_t, 1)
                pool.wait_ge(tT_sb, i + 1)
                nc.gpsimd.tensor_copy(ltT[0:TW, ds(i * P, P)], trowT[0:TW, :]).then_inc(kept_tT, 1)

            pool.wait_ge(s_hot, 1)
            residual(0, False)
            residual(1, True)
            residual_c(0, False)
            residual_c(1, True)
            pool.wait_ge(s_zero, 1)
            nc.gpsimd.iota(tok_id[:, :], pattern=[[P, NT + 1]], base=0, channel_multiplier=1).then_inc(s_id, 1)
            pool.wait_ge(s_id, 1)
            nc.gpsimd.tensor_copy(lrows[:, 0, ID_COL:ID_COL + 1].bitcast(i32), tok_id[:, NT:NT + 1]).then_inc(s_id, 1)
            pool.wait_ge(s_id, 2)
            pool.dma_start(slot_rows.rearrange("(t p) n -> p t n", p=P),
                           zeros.unsqueeze(1).to_broadcast([P, NS, TWP])).then_inc(d_zero, 16)
            pool.dma_start(out_rows[TOK:TOK + P, :], lrows[:, :, :].rearrange("p t n -> p (t n)")[:, TWP:TWP + D]
                           ).then_inc(d_dummy, 16)
            pool.wait_ge(d_zero, 16)
            pool.wait_ge(d_dummy, 16)
            nc.gpsimd.tensor_copy(lrows[:, :, ID_COL:ID_COL + 1].rearrange("p t o -> p (t o)").bitcast(i32),
                                  tok_id[:, 0:NT]).then_inc(s_id, 1)
            nc.gpsimd.memset(lrows[:, :, TW - 1:TW], 1.0).then_inc(s_id, 1)
            nc.gpsimd.tensor_copy(lrows[:, :, NLR:NLR + NLANG], lang_hot).then_inc(s_id, 1)

            def tile_steps(i, odd, last=False):
                if not last:
                    residual(i + 1, not odd)
                    residual_c(i + 1, not odd)
                keep(i - 1)

            tile_steps(1, True)
            tile_steps(2, False)
            with pool.Fori(0, NE) as e:
                tile_steps(2 * e + 3, True)
                tile_steps(2 * e + 4, False)
            for i in range(2 * NE + 3, NT):
                tile_steps(i, i % 2 == 1, last=(i == NT - 1))
            keep(NT - 1)

            pool.wait_ge(kept_t, NT)
            pool.wait_ge(s_id, 5)
            pool.wait_ge(r_gates, 1)
            for k in range(2):
                pool.wait_ge(r_slots, k + 1)
                nc.gpsimd.tensor_copy(lrows[:, :, W_COL:W_COL + 1].rearrange("p t o -> p (t o)"),
                                      gate[:, k, :]).then_inc(gate_col, 1)
                pool.wait_ge(gate_col, k + 1)
                for i in range(NT):
                    pool.indirect_dma_start(slot_rows, bass.IndirectOffsetOnAxis(slot[:, k, i:i + 1], 0),
                                            lrows[:, i, :], None).then_inc(d_scatter, 16)
                pool.wait_ge(d_scatter, 16 * NT * (k + 1))

            def add_rows(t, s):
                pool.wait_ge(y_ok, t + 1)
                if t > 0:
                    pool.wait_ge(d_add, 16 * t)
                pool.wait_ge(d_dummy, 16)
                pool.indirect_dma_start(out_rows,
                                        bass.IndirectOffsetOnAxis(s_row[s][:, ID_COL:ID_COL + 1].bitcast(u32), 0),
                                        y_sb[t % YR], None, compute_op=ALU.add).then_inc(d_add, 16)

            pool.wait_ge(r_done, 1)
            pool.wait_ge(sh_ps, 4 * (TOK // U))
            for t in range(2):
                copy_first(pool, nc.gpsimd.tensor_copy, t, t, 2)
            for v in range(2):
                pool.wait_ge(d_out[v], 16 * NT // 2)
            for t in range(NS):
                if t + 2 < NS:
                    pool.wait_ge(h_ps, 3 * t + 3)
                    copy_first(pool, nc.gpsimd.tensor_copy, t + 2, t, 2)
                add_rows(t, t % RING)
            pool.wait_ge(d_add, 16 * NS)

        @block.scalar
        def _(act):
            copy = nc.scalar.copy
            for dst, src in loads[1::2]:
                with nc.allow_non_contiguous_dma(reason="a few hundred words of biases, embeddings and ids"):
                    act.dma_start(dst, src).then_inc(d_setup, 16)

            def merge_copy(n, dst):
                act.wait_ge(merge_ps, n + 1)
                copy(dst, ps[0:NLR + NLANG, 6, :]).then_inc(merge_sb, 1)

            act.wait_ge(s_sp1, 1)
            copy(aT, ps[:, 0, 0:KC * NLR].rearrange("p (c n) -> p c n", c=KC))
            copy(wr[0:NLR + NLANG, :], ps[0:NLR + NLANG, 0, 256:256 + NE]).then_inc(s_sp1c, 1)
            act.wait_ge(s_sp1, 2)
            nc.scalar.mul(bT, ps[0:LR, 2:4, :].rearrange("p t (n m) -> p (t n) m", m=D), 1.0 / LR).then_inc(s_bT, 1)
            for n in range(4):
                act.wait_ge(s_mrg, n + 1)
                src = ps[:, n, :].rearrange("p (c n) -> p c n", c=KC)
                if n < 3:
                    copy(wm[n], src).then_inc(s_mrgc, 1)
                else:
                    nc.scalar.activation(wm[n], src, ACT.Copy, scale=rz).then_inc(s_mrgc, 1)
            act.wait_ge(s_hot, 1)

            def xT_copy(i):
                act.wait_ge(xT_ps, i + 1)
                copy(xT, ps[:, 5, 0:D].rearrange("p (c n) -> p c n", c=KC)).then_inc(xT_sb, 1)

            def cT_copy(i):
                act.wait_ge(cT_ps, i + 1)
                copy(cT, ps[:, 5, 0:D].rearrange("p (c n) -> p c n", c=KC)).then_inc(cT_sb, 1)

            def q_copy(i):
                act.wait_ge(q_ps, i + 1)
                for m in range(KC):
                    last = nc.scalar.activation(qT[:, m, :], ps[:, 5, D + m * P:D + (m + 1) * P], ACT.Identity,
                                                bias=bq_quarter[:, m:m + 1], scale=0.25)
                last.then_inc(q_sb, 1)

            def exps(i):
                act.wait_ge(shift_sb, i + 1)
                nc.scalar.activation(probs, probs, ACT.Exp).then_inc(prob_sb, 1)

            def pT_copy(i):
                act.wait_ge(pT_ps, 2 * i + 1)
                copy(probsT[:, 0:4, :].rearrange("p a n -> p (a n)"), ps[:, 0, :]).then_inc(pTa_sb, 1)

            def oT_copy(i):
                act.wait_ge(oT_ps, i + 1)
                copy(oT, ps[:, 7, 0:D].rearrange("p (c n) -> p c n", c=KC)).then_inc(oT_sb, 1)

            def x2T_copy(i):
                act.wait_ge(x2T_ps, i + 1)
                copy(x2T, ps[:, 7, 0:D].rearrange("p (c n) -> p c n", c=KC)).then_inc(x2T_sb, 1)

            def tT_copy(i):
                act.wait_ge(tT_ps, i + 1)
                if not isinstance(i, int) or i > 0:
                    act.wait_ge(kept_tT, i)
                copy(trowT[0:TW, :], ps[0:TW, 7, 0:P]).then_inc(tT_sb, 1)

            def expert_cols(e, j):
                return 3 * e + (2 + j), w1m[0:NLR + NLANG, w1_cols(e, j)]

            def tile_steps(i, first=False, merge_a=None, merge_b=None):
                one_more, two_more = not isinstance(i, int) or i + 1 < NT, not isinstance(i, int) or i + 2 < NT
                if one_more:
                    cT_copy(i + 1)
                if not first:
                    oT_copy(i - 1)
                if merge_a:
                    merge_copy(*merge_a)
                exps(i)
                if one_more:
                    q_copy(i + 1)
                pT_copy(i)
                if not first:
                    x2T_copy(i - 1)
                if two_more:
                    xT_copy(i + 2)
                if merge_b:
                    merge_copy(*merge_b)
                if not first:
                    tT_copy(i - 1)

            xT_copy(0)
            cT_copy(0)
            q_copy(0)
            xT_copy(1)
            tile_steps(0, first=True)
            for j in range(HS // CH):
                at_col = NE * EW + j * 2 * CH
                tile_steps(1 + j, merge_b=(j, w1m[0:NLR + NLANG, at_col:at_col + 2 * CH]))
            with act.Fori(0, NE) as e:
                i = 2 * e + 3
                tile_steps(i, merge_a=expert_cols(e, 0), merge_b=expert_cols(e, 1))
                tile_steps(i + 1, merge_b=expert_cols(e, 2))
            for i in range(2 * NE + 3, NT):
                tile_steps(i)
            oT_copy(NT - 1)
            x2T_copy(NT - 1)
            tT_copy(NT - 1)

            def shared_gelu(u):
                for c in range(4):
                    act.wait_ge(sh_ps, 4 * u + (c + 1))
                    nc.scalar.activation(sh_g[c % 2], ps[:, 2 * (c % 2) + 1, 0:U], ACT.Gelu).then_inc(shg_ok, 1)

            shared_gelu(0)
            shared_gelu(1)
            act.wait_ge(r_gap, 1)
            nc.scalar.activation(r_d, r_d, ACT.Exp).then_inc(r_exp, 1)
            shared_gelu(2)
            with act.Fori(3, TOK // U) as u:
                shared_gelu(u)

            def gelus(t, s, more=True):
                for j in range(NJ):
                    act.wait_ge(h_ps, 3 * t + (j + 1))
                    nc.scalar.activation(g_sb[j], ps[:, j, CH:2 * CH], ACT.Gelu).then_inc(g_ok, 1)
                    if j == 0 and more:
                        copy_first(act, copy, t + 2, s, 0)

            act.wait_ge(r_done, 1)
            act.wait_ge(sh_ps, 4 * (TOK // U))
            for t in range(2):
                copy_first(act, copy, t, t, 0)
            with act.Fori(0, NS // 2 - 1) as w:
                for s in range(2):
                    gelus(2 * w + s, s)
            for t in range(2 * (NS // 2 - 1), NS):
                gelus(t, t, more=t + 2 < NS)

        @block.vector
        def _(dve):
            links = [0]

            def link(ins):
                links[0] += 1
                ins.then_inc(chain, 1)
                dve.wait_ge(chain, links[0])

            V = nc.vector
            dve.wait_ge(d_setup, ALL_SETUP)
            V.tensor_copy(ali, ali_f).then_inc(s_const, 1)
            V.tensor_copy(tri_b[:, :], col["tri"]).then_inc(s_const, 1)
            link(V.tensor_copy(lang_f, lang_i[:, :]))
            for lang in range(NLANG):
                V.tensor_scalar(lang_hot[:, :, lang], lang_f, float(lang), None, ALU.is_equal)
            dve.wait_ge(s_zero, 3)
            for s in range(2):
                for h in range(2):
                    V.tensor_copy(vD[s][:, :, :, 32 + h],
                                  col["kv"][:, h:h + 1].unsqueeze(2).to_broadcast([P, 2, 8]))
            V.tensor_scalar(bq_quarter, bq_col, 0.25, None, ALU.mult)
            V.tensor_scalar(bo_rz, bo_bc, rz, None, ALU.mult).then_inc(s_hot, 1)
            dve.wait_ge(s_hot, 1)

            def c_add(i, odd):
                s = int(odd)
                dve.wait_ge(c_ps, i + 1)
                dve.wait_ge(d_cb[s], 2 * turn(i, odd))
                if not isinstance(i, int) or i > 0:
                    dve.wait_ge(xres_sb, i)
                V.tensor_tensor(c_sb, ps[:, 5, 0:D], cond_bias[s], ALU.add).then_inc(c_ok, 1)

            def k_spread(i):
                dve.wait_ge(kv_ps, i + 1)
                for m in range(KC):
                    last = V.scalar_tensor_tensor(
                        out=kD[:, m], in0=ps[:, 4, m * P:(m + 1) * P].unsqueeze(1).to_broadcast([P, 2, P]),
                        scalar=bk_col[:, m:m + 1], in1=col["kmask"].unsqueeze(2).to_broadcast([P, 2, P]),
                        op0=ALU.add, op1=ALU.mult)
                last.then_inc(k_sb, 1)

            def v_spread(i, odd):
                for h in range(2):
                    r = slice(h * S, (h + 1) * S)
                    last = V.tensor_tensor(
                        vD[int(odd)][r, :, :, h * HD:(h + 1) * HD],
                        ps[r, 4, D:2 * D].rearrange("p (b h d) -> p b h d", b=2, d=HD),
                        bv_half[r, :].rearrange("p (h d) -> p h d", d=HD).unsqueeze(1).to_broadcast([S, 2, 8, HD]),
                        ALU.add)
                last.then_inc(v_sb, 1)

            scores = ps[:, 0:4, 0:256].rearrange("p g (h k) -> p g h k", k=S)

            def shift(i):
                dve.wait_ge(s_ps, i + 1)
                V.tensor_reduce(smax.rearrange("p (g h) -> p g h", g=4), scores, AX.X, ALU.max).then_inc(max_sb, 1)
                dve.wait_ge(max_sb, i + 1)
                if not isinstance(i, int) or i > 0:
                    dve.wait_ge(pT_ps, 2 * i)
                V.tensor_tensor(probs.rearrange("p (g h k) -> p g h k", g=4, k=S), scores,
                                smax.rearrange("p (g h) -> p g h", g=4).unsqueeze(3).to_broadcast([P, 4, 4, S]),
                                ALU.subtract).then_inc(shift_sb, 1)

            def pT_copy(i):
                dve.wait_ge(pT_ps, 2 * i + 2)
                V.tensor_copy(probsT[:, 4:8, :].rearrange("p a n -> p (a n)"), ps[:, 1, :]).then_inc(pTv_sb, 1)

            o_acc = ps[:, 2, 0:8 * 34].rearrange("p (a n) -> p a n", n=34)

            def normalize(i):
                dve.wait_ge(o_ps, i + 1)
                V.reciprocal(rsum.rearrange("p (a h) -> p a h", h=2), o_acc[:, :, 32:34]).then_inc(rsum_sb, 1)
                dve.wait_ge(rsum_sb, i + 1)
                V.tensor_tensor(onorm.rearrange("p (a h d) -> p a h d", h=2, d=HD),
                                o_acc[:, :, 0:32].rearrange("p a (h d) -> p a h d", h=2),
                                rsum.rearrange("p (a h) -> p a h", h=2).unsqueeze(3).to_broadcast([P, 8, 2, HD]),
                                ALU.mult).then_inc(o_sb, 1)

            def x2_add(i, odd):
                s = int(odd)
                dve.wait_ge(att_ps, i + 1)
                dve.wait_ge(xres_sb, i + 1)
                if not (isinstance(i, int) and i < 2):
                    dve.wait_ge(d_x2[s], turn(i, odd) - 16)
                V.tensor_tensor(x2[s], ps[:, 7, 0:D], x_res[s], ALU.add).then_inc(x2_sb, 1)

            def t_mask(i):
                dve.wait_ge(t_ps, i + 1)
                if not isinstance(i, int) or i > 0:
                    dve.wait_ge(kept_t, i)
                hot = lang_hot[:, ds(i, 1), :].rearrange("p o l -> p (o l)")
                V.tensor_tensor(trow[:, 0:NLR].rearrange("p (l r) -> p l r", l=NLANG),
                                ps[:, 7, 0:NLR].rearrange("p (l r) -> p l r", l=NLANG),
                                hot.unsqueeze(2).to_broadcast([P, NLANG, RANK]), ALU.mult)
                V.tensor_copy(trow[:, NLR:NLR + NLANG], hot).then_inc(t_sb, 1)

            def logit_copy(i):
                dve.wait_ge(lg_ps, i + 1)
                V.tensor_scalar(logits[:, ds(i, 1), :].rearrange("p o n -> p (o n)"), ps[:, 7, 0:NE], 1.0 / TAU, None,
                                ALU.mult).then_inc(lg_sb, 1)

            def tile_steps(i, odd, first=False):
                one_more, two_more = not isinstance(i, int) or i + 1 < NT, not isinstance(i, int) or i + 2 < NT
                shift(i)
                if one_more:
                    k_spread(i + 1)
                    v_spread(i + 1, not odd)
                if not first:
                    x2_add(i - 1, not odd)
                pT_copy(i)
                if not first:
                    t_mask(i - 1)
                normalize(i)
                if two_more:
                    c_add(i + 2, odd)
                if not first:
                    logit_copy(i - 1)

            c_add(0, False)
            k_spread(0)
            v_spread(0, False)
            c_add(1, True)
            tile_steps(0, False, first=True)
            tile_steps(1, True)
            tile_steps(2, False)
            with dve.Fori(0, NE) as e:
                tile_steps(2 * e + 3, True)
                tile_steps(2 * e + 4, False)
            for i in range(2 * NE + 3, NT):
                tile_steps(i, i % 2 == 1)
            x2_add(NT - 1, True)
            t_mask(NT - 1)
            logit_copy(NT - 1)

            down = col["count_down"].unsqueeze(1).to_broadcast([P, NT, NE])

            def over_e(x):
                return x.unsqueeze(2).to_broadcast([P, NT, NE])

            def largest(cur, top, hot):
                link(V.tensor_reduce(top, cur, AX.X, ALU.max))
                link(V.tensor_tensor(r_b, cur, over_e(top), ALU.is_equal))
                link(V.tensor_tensor(r_b, r_b, down, ALU.mult))
                link(V.tensor_reduce(r_s, r_b, AX.X, ALU.max))
                link(V.tensor_tensor(hot, r_b, over_e(r_s), ALU.is_equal))

            def without_first():
                link(V.scalar_tensor_tensor(out=r_a, in0=r_m1, scalar=NEG, in1=logits[:, :, :],
                                            op0=ALU.mult, op1=ALU.add))

            def chosen_experts():
                V.tensor_tensor(chosen.rearrange("p (t e) -> p t e", e=NE), r_m1, r_m2, ALU.add).then_inc(r_chosen, 1)
                V.tensor_tensor(r_d, r_max2, r_max1, ALU.subtract).then_inc(r_gap, 1)

            def expert_bases():
                dve.wait_ge(r_rank, 1)
                link(V.tensor_reduce(r_n, ps[:, 7, 0:NT * NE].rearrange("p (t e) -> p e t", e=NE), AX.X, ALU.add))
                link(V.tensor_tensor(r_cmp, r_n.unsqueeze(2).to_broadcast([P, NE, NT]),
                                     col["tile_start"].unsqueeze(1).to_broadcast([P, NE, NT]), ALU.is_gt))
                link(V.tensor_reduce(r_tiles, r_cmp, AX.X, ALU.add))
                link(V.tensor_scalar(r_one, r_tiles, 0.0, 1.0, ALU.mult, ALU.add))
                link(V.tensor_tensor_scan(r_end, r_one, r_tiles, 0.0, ALU.mult, ALU.add))
                link(V.tensor_tensor(r_base, r_end, r_tiles, ALU.subtract))

            def slot_bases():
                link(V.scalar_tensor_tensor(out=r_a, in0=r_base.unsqueeze(1).to_broadcast([P, NT, NE]),
                                            scalar=float(P), in1=ps[:, 6, 0:NT * NE].rearrange("p (t e) -> p t e", e=NE),
                                            op0=ALU.mult, op1=ALU.add))

            def slots(k, hot):
                link(V.tensor_tensor(r_b, hot, r_a, ALU.mult))
                link(V.tensor_reduce(r_s, r_b, AX.X, ALU.add))
                V.tensor_copy(slot[:, k, :], r_s).then_inc(r_slots, 1)
                dve.wait_ge(r_slots, k + 1)

            def gates():
                dve.wait_ge(r_exp, 1)
                link(V.tensor_scalar(r_s, r_d, 1.0, None, ALU.add))
                link(V.reciprocal(gate[:, 0, :], r_s))
                V.tensor_tensor(gate[:, 1, :], gate[:, 0, :], r_d, ALU.mult).then_inc(r_gates, 1)

            def tile_experts():
                link(V.tensor_tensor(r_et, r_base.unsqueeze(1).to_broadcast([P, NS, NE]),
                                     col["slot_tile"].unsqueeze(2).to_broadcast([P, NS, NE]), ALU.is_le))
                link(V.tensor_reduce(r_ef, r_et, AX.X, ALU.add))
                V.tensor_scalar(expert_of[:, :], r_ef[0:1, :], -1.0, None, ALU.add).then_inc(r_done, 1)

            def sh_multiply(u, half):
                for c in range(4):
                    dve.wait_ge(shg_ok, 4 * u + (c + 1))
                    V.tensor_tensor(sh_aT[half][:, c, :], ps[:, 2 * (c % 2), 0:U], sh_g[c % 2],
                                    ALU.mult).then_inc(sha_ok, 1)

            def combine(u, v, half):
                n = 2 * u + v
                dve.wait_ge(d_cx[v], 16 * u + 16)
                V.tensor_tensor(c_x2[v], c_x2[v], bs2_bc[:, :], ALU.add).then_inc(bs2_ok, 1)
                dve.wait_ge(bs2_ok, n + 1)
                dve.wait_ge(shy_ps, n + 1)
                V.tensor_tensor(c_x2[v], c_x2[v], ps[:, 4 + v, half * D:(half + 1) * D], ALU.add).then_inc(comb_ok, 1)

            dve.wait_ge(lg_sb, NT)
            largest(logits[:, :, :], r_max1, r_m1)
            sh_multiply(0, 0)
            without_first()
            largest(r_a, r_max2, r_m2)
            chosen_experts()
            sh_multiply(1, 1)
            for v in range(2):
                combine(0, v, 0)
            sh_multiply(2, 0)
            expert_bases()
            slot_bases()
            for v in range(2):
                combine(1, v, 1)
            sh_multiply(3, 1)
            slots(0, r_m1)
            for v in range(2):
                combine(2, v, 0)
            gates()
            sh_multiply(4, 0)
            slots(1, r_m2)
            for v in range(2):
                combine(3, v, 1)
            sh_multiply(5, 1)
            for v in range(2):
                combine(4, v, 0)
            tile_experts()
            sh_multiply(6, 0)
            for v in range(2):
                combine(5, v, 1)

            def shared_two(w, last=False):
                sh_multiply(2 * w + 1, 1)
                for v in range(2):
                    combine(2 * w, v, 0)
                if not last:
                    sh_multiply(2 * w + 2, 0)
                for v in range(2):
                    combine(2 * w + 1, v, 1)

            with dve.Fori(3, TOK // U // 2 - 1) as w:
                shared_two(w)
            shared_two(TOK // U // 2 - 1, last=True)

            def rowT_copy(t, s):
                dve.wait_ge(rowT_ps, t + 1)
                V.tensor_copy(s_rowT[s % 2][0:TW, :], ps[0:TW, 7, 0:P]).then_inc(rowT_sb, 1)

            def multiply(n, j):
                dve.wait_ge(g_ok, n + 1)
                V.tensor_tensor(actT_sb[j].rearrange("p c n -> p (c n)"), ps[:, j, 0:CH], g_sb[j],
                                ALU.mult).then_inc(act_ok, 1)

            def gate_bias(t, s):
                e = dve.value_load(expert_of[0:1, ds(t, 1)], min_val=0, max_val=NE - 1)
                V.tensor_scalar(gated_be2[s % 2], be2_bc[:, ds(e * D, D)], s_row[s][:, W_COL:W_COL + 1], None,
                                ALU.mult).then_inc(gb_ok, 1)

            def add_bias(t, s):
                dve.wait_ge(y_ps, t + 1)
                dve.wait_ge(gb_ok, t + 1)
                if not (isinstance(t, int) and t < YR):
                    dve.wait_ge(d_add, 16 * t - 16 * (YR - 1))
                V.scalar_tensor_tensor(out=y_sb[s % YR], in0=ps[:, 3 + s % 2, 0:D],
                                       scalar=s_row[s][:, W_COL:W_COL + 1], in1=gated_be2[s % 2],
                                       op0=ALU.mult, op1=ALU.add).then_inc(y_ok, 1)

            def routed_tiles(q, first=False, last=False):
                for s in range(NS % RING if last else RING):
                    t = RING * q + s
                    multiply(3 * t, 0)
                    if not (last and s == NS % RING - 1):
                        rowT_copy(t + 1, (s + 1) % RING)
                    multiply(3 * t + 1, 1)
                    if not last or s + 2 < NS % RING:
                        copy_first(dve, V.tensor_copy, t + 2, s, 1)
                    if not (first and s == 0):
                        add_bias(t - 1, (s - 1) % RING)
                    gate_bias(t, s)
                    multiply(3 * t + 2, 2)

            dve.wait_ge(r_done, 1)
            dve.wait_ge(sh_ps, 4 * (TOK // U))
            for t in range(2):
                copy_first(dve, V.tensor_copy, t, t, 1)
            rowT_copy(0, 0)
            dve.wait_ge(d_be2, 16)
            routed_tiles(0, first=True)
            with dve.Fori(1, NS // RING) as q:
                routed_tiles(q)
            routed_tiles(NS // RING, last=True)
            add_bias(NS - 1, (NS - 1) % RING)

        @block.tensor
        def _(pe):
            mm, tr = nc.tensor.matmul, nc.tensor.transpose
            pe.wait_ge(d_setup, ALL_SETUP)
            pe.wait_ge(s_const, 2)
            for c in range(KC):
                tr(ps[:, 0, c * NLR:(c + 1) * NLR], lora_a[:, c * P:(c + 1) * P], ident[0:NLR, 0:NLR])
            for c in range(KC):
                last = mm(ps[0:NLR + NLANG, 0, 256:256 + NE], ba[:, c, :], wr_raw[:, c, :], start=(c == 0),
                          stop=(c == KC - 1))
            last.then_inc(s_sp1, 1)
            for n in range(4):
                for m in range(KC):
                    last = mm(ps[0:LR, 2 + n // 2, (n % 2) * D + m * P:(n % 2) * D + (m + 1) * P], b_raw[n][:, m, :],
                              ident, start=True, stop=True)
            last.then_inc(s_sp1, 1)
            pe.wait_ge(s_bT, 1)
            pe.wait_ge(s_sp1c, 1)
            for n in range(4):
                for k in range(KC):
                    mm(ps[:, n, k * D:(k + 1) * D], a_raw[n][:, k * P:(k + 1) * P], bT[:, n, :],
                       start=True, stop=False)
                    for m in range(KC):
                        last = mm(ps[:, n, k * D + m * P:k * D + (m + 1) * P],
                                  w_raw[n][:, m, k * P:(k + 1) * P], ident, start=False, stop=(m == KC - 1))
                last.then_inc(s_mrg, 1)
            pe.wait_ge(s_mrgc, 4)
            pe.wait_ge(s_zero, 4)

            def x_transpose(i, odd):
                s = int(odd)
                pe.wait_ge(d_x[s], turn(i, odd))
                if not isinstance(i, int) or i > 0:
                    pe.wait_ge(q_sb, i)
                for c in range(KC):
                    last = tr(ps[:, 5, c * P:(c + 1) * P], x_in[s][:, c * P:(c + 1) * P], ident)
                last.then_inc(xT_ps, 1)

            def condition(i, odd):
                s = int(odd)
                pe.wait_ge(d_cw[s], 2 * turn(i, odd))
                pe.wait_ge(xT_sb, i + 1)
                for b in range(2):
                    for k in range(KC):
                        last = mm(ps[b * S:(b + 1) * S, 5, 0:D], xT[:, k, b * S:(b + 1) * S],
                                  cond_w[s][:, b, k, :], start=(k == 0), stop=(k == KC - 1))
                last.then_inc(c_ps, 1)

            def c_transpose(i):
                pe.wait_ge(c_ok, i + 1)
                for c in range(KC):
                    last = tr(ps[:, 5, c * P:(c + 1) * P], c_sb[:, c * P:(c + 1) * P], ident)
                last.then_inc(cT_ps, 1)

            def project(i):
                pe.wait_ge(cT_sb, i + 1)
                if not isinstance(i, int) or i > 0:
                    pe.wait_ge(k_sb, i)
                    pe.wait_ge(v_sb, i)

                def transposed(w, bank, at):
                    for m in range(KC):
                        for k in range(KC):
                            last = mm(ps[:, bank, at + m * P:at + (m + 1) * P], wm[w][:, k, m * P:(m + 1) * P], cT[:, k, :],
                                      start=(k == 0), stop=(k == KC - 1))
                    return last

                transposed(1, 4, 0)
                wv = [wm[2][:, k, :].rearrange("p (h two d) -> p two h d", two=2, d=HD) for k in range(KC)]
                for b in range(2):
                    for h in range(2):
                        for k in range(KC):
                            last = mm(ps[h * S:(h + 1) * S, 4, D + b * P:D + (b + 1) * P].rearrange(
                                "p (h d) -> p h d", d=HD), cT[:, k, b * S:(b + 1) * S], wv[k][:, h],
                                start=(k == 0), stop=(k == KC - 1))
                last.then_inc(kv_ps, 1)
                transposed(0, 5, D).then_inc(q_ps, 1)

            def score(i):
                pe.wait_ge(q_sb, i + 1)
                pe.wait_ge(k_sb, i + 1)
                if not isinstance(i, int) or i > 0:
                    pe.wait_ge(pTa_sb, i)
                    pe.wait_ge(pTv_sb, i)
                    pe.wait_ge(o_sb, i)
                for g in range(4):
                    mm(ps[:, g, 0:256], ali[:, 0:P], ali[:, P + g * 256:P + (g + 1) * 256], start=True, stop=False)
                for m in range(KC):
                    for b in range(2):
                        for g in range(4):
                            r = slice(32 * g, 32 * g + 32)
                            last = mm(ps[b * S:(b + 1) * S, g, m * P:(m + 1) * P].rearrange("p (h k) -> p h k", h=2),
                                      qT[r, m, b * S:(b + 1) * S], kD[r, m, :, b * S:(b + 1) * S],
                                      start=False, stop=(m == KC - 1))
                last.then_inc(s_ps, 1)

            def prob_transpose(i):
                pe.wait_ge(prob_sb, i + 1)
                for n in range(8):
                    last = tr(ps[:, n // 4, (n % 4) * P:(n % 4 + 1) * P], probs[:, n * P:(n + 1) * P], ident)
                    if n % 4 == 3:
                        last.then_inc(pT_ps, 1)

            def attend(i, odd):
                pe.wait_ge(pTa_sb, i + 1)
                pe.wait_ge(pTv_sb, i + 1)
                pe.wait_ge(v_sb, i + 1)
                for g in range(4):
                    for m in range(KC):
                        hp = 4 * m + g
                        for b in range(2):
                            last = mm(ps[b * S:(b + 1) * S, 2, hp * 34:(hp + 1) * 34],
                                      probsT[:, 2 * g + m, b * S:(b + 1) * S], vD[int(odd)][:, b, hp, :],
                                      start=True, stop=True)
                last.then_inc(o_ps, 1)

            def o_transpose(i):
                pe.wait_ge(o_sb, i + 1)
                if not isinstance(i, int) or i > 0:
                    pe.wait_ge(lg_sb, i)
                for c in range(KC):
                    last = tr(ps[:, 7, c * P:(c + 1) * P], onorm[:, c * P:(c + 1) * P], ident)
                last.then_inc(oT_ps, 1)

            def output(i):
                pe.wait_ge(oT_sb, i + 1)
                for k in range(KC):
                    last = mm(ps[:, 7, 0:D], oT[:, k, :], wm[3][:, k, :], start=(k == 0), stop=(k == KC - 1))
                last.then_inc(att_ps, 1)

            def x2_transpose(i, odd):
                pe.wait_ge(x2_sb, i + 1)
                for c in range(KC):
                    last = tr(ps[:, 7, c * P:(c + 1) * P], x2[int(odd)][:, c * P:(c + 1) * P], ident)
                last.then_inc(x2T_ps, 1)

            def low_rank(i):
                pe.wait_ge(x2T_sb, i + 1)
                for c in range(KC):
                    last = mm(ps[:, 7, 0:NLR], x2T[:, c, :], aT[:, c, :], start=(c == 0), stop=(c == KC - 1))
                last.then_inc(t_ps, 1)

            def row_transpose(i):
                pe.wait_ge(t_sb, i + 1)
                tr(ps[0:TW, 7, 0:P], trow[:, 0:TW], ident).then_inc(tT_ps, 1)

            def router(i):
                pe.wait_ge(tT_sb, i + 1)
                mm(ps[:, 7, 0:NE], trowT[0:TW, :], wr[0:TW, :], start=True, stop=True).then_inc(lg_ps, 1)

            def merge(n, j, arrived):
                pe.wait_ge(d_stage[j], arrived)
                if not isinstance(n, int) or n > 0:
                    pe.wait_ge(merge_sb, n)
                for c in range(KC):
                    last = mm(ps[0:NLR + NLANG, 6, :], ba[:, c, :], stage_w[j][:, c, :],
                              start=(c == 0), stop=(c == KC - 1))
                last.then_inc(merge_ps, 1)

            def tile_steps(i, odd, first=False, merge_a=None, merge_b=None):
                one_more, two_more = not isinstance(i, int) or i + 1 < NT, not isinstance(i, int) or i + 2 < NT
                score(i)
                if one_more:
                    c_transpose(i + 1)
                if not first:
                    o_transpose(i - 1)
                if merge_a:
                    merge(*merge_a)
                if one_more:
                    project(i + 1)
                if not first:
                    output(i - 1)
                prob_transpose(i)
                if not first:
                    x2_transpose(i - 1, not odd)
                if two_more:
                    x_transpose(i + 2, odd)
                if merge_b:
                    merge(*merge_b)
                if not first:
                    low_rank(i - 1)
                attend(i, odd)
                if not first:
                    row_transpose(i - 1)
                if two_more:
                    condition(i + 2, odd)
                if not first:
                    router(i - 1)

            x_transpose(0, False)
            condition(0, False)
            c_transpose(0)
            project(0)
            x_transpose(1, True)
            condition(1, True)
            tile_steps(0, False, first=True)
            tile_steps(1, True, merge_b=(0, 0, 32))
            tile_steps(2, False, merge_b=(1, 1, 32))
            with pe.Fori(0, NE) as e:
                i = 2 * e + 3
                tile_steps(i, True, merge_a=(3 * e + 2, 0, 32 * e + 64), merge_b=(3 * e + 3, 1, 32 * e + 64))
                tile_steps(i + 1, False, merge_b=(3 * e + 4, 2, 32 * e + 32))
            for i in range(2 * NE + 3, NT):
                tile_steps(i, i % 2 == 1)
            o_transpose(NT - 1)
            output(NT - 1)
            x2_transpose(NT - 1, True)
            low_rank(NT - 1)
            row_transpose(NT - 1)
            router(NT - 1)

            def hidden(u):
                for c in range(4):
                    for g in range(2):
                        at_col = NE * EW + (c // 2) * 2 * CH + g * CH + (c % 2) * P
                        if g == 0 and not (isinstance(u, int) and u == 0 and c < 2):
                            pe.wait_ge(sha_ok, 4 * u + (c - 1))
                        last = mm(ps[:, 2 * (c % 2) + g, 0:U], w1m[0:TW, at_col:at_col + P],
                                  ltT[0:TW, ds(u * U, U)], start=True, stop=True)
                    last.then_inc(sh_ps, 1)

            def shared_out(u, half):
                pe.wait_ge(sha_ok, 4 * u + 4)
                for v in range(2):
                    if not (isinstance(u, int) and u == 0):
                        pe.wait_ge(comb_ok, 2 * u + (v - 1))
                    for k in range(HS // P):
                        last = mm(ps[:, 4 + v, half * D:(half + 1) * D], sh_aT[half][:, k, v * P:(v + 1) * P],
                                  ws2[:, k, :], start=(k == 0), stop=(k == HS // P - 1))
                    last.then_inc(shy_ps, 1)

            def ranks():
                pe.wait_ge(r_chosen, 1)
                n = NT * NE
                mm(ps[:, 6, 0:n], tri_b[:, :], chosen, start=True, stop=False)
                for back in range(1, NT):
                    mm(ps[:, 6, back * NE:n], ones_b[:, :], chosen[:, 0:n - back * NE], start=False,
                       stop=(back == NT - 1))
                mm(ps[:, 7, 0:n], ones_b[:, :], chosen, start=True, stop=True).then_inc(r_rank, 1)

            def shared_two(w, first=False):
                hidden(2 * w + 1)
                shared_out(2 * w, 0)
                hidden(2 * w + 2)
                if first:
                    ranks()
                shared_out(2 * w + 1, 1)

            pe.wait_ge(kept_tT, NT)
            pe.wait_ge(d_w1bias, 16 * len(be1_rows))
            pe.wait_ge(merge_sb, n_merge)
            hidden(0)
            pe.wait_ge(d_ws2, 16)
            shared_two(0, first=True)
            with pe.Fori(1, TOK // U // 2 - 1) as w:
                shared_two(w)
            hidden(TOK // U - 1)
            shared_out(TOK // U - 2, 0)
            shared_out(TOK // U - 1, 1)

            def rows_transpose(t, s, arrived):
                pe.wait_ge(d_row[s], arrived)
                if not isinstance(t, int) or t > 0:
                    pe.wait_ge(rowT_sb, t)
                tr(ps[0:TW, 7, 0:P], s_row[s][:, 0:TW], ident).then_inc(rowT_ps, 1)

            def first_layer(t, s, j):
                if j == 0:
                    pe.wait_ge(rowT_sb, t + 1)
                pe.wait_ge(w1x_ok[j], t + 1)
                for g in range(2):
                    for c in range(2):
                        at = g * CH + c * P
                        last = mm(ps[:, j, at:at + P], w1x[s % 2][:, j * 2 * CH + at:j * 2 * CH + at + P],
                                  s_rowT[s % 2][0:TW, :], start=True, stop=True)
                last.then_inc(h_ps, 1)

            def second_layer(t, s, j, e):
                pe.wait_ge(act_ok, 3 * t + (j + 1))
                if j == 0 and not (isinstance(t, int) and t < 2):
                    pe.wait_ge(y_ok, t - 1)
                for c in range(2):
                    last = mm(ps[:, 3 + s % 2, 0:D], actT_sb[j][:, c, :], arena[:, ds(e * E2 + (2 * j + c) * D, D)],
                              start=(j == 0 and c == 0), stop=(j == NJ - 1 and c == 1))
                if j == NJ - 1:
                    last.then_inc(y_ps, 1)

            def expert(t):
                return pe.value_load(expert_of[0:1, ds(t, 1)], min_val=0, max_val=NE - 1)

            def routed_tiles(q, last=False):
                for s in range(NS % RING if last else RING):
                    t = RING * q + s
                    after, more = (s + 1) % RING, not (last and s == NS % RING - 1)
                    if more:
                        rows_transpose(t + 1, after, 16 * q + (32 if after == 0 else 16))
                    first_layer(t, s, 2)
                    e = expert(t)
                    for j in range(NJ):
                        second_layer(t, s, j, e)
                        if j < NJ - 1 and more:
                            first_layer(t + 1, after, j)

            pe.wait_ge(d_w2, 16 * NE)
            pe.wait_ge(r_done, 1)
            pe.wait_ge(comb_ok, NT)
            rows_transpose(0, 0, 16)
            first_layer(0, 0, 0)
            first_layer(0, 0, 1)
            routed_tiles(0)
            with pe.Fori(1, NS // RING) as q:
                routed_tiles(q)
            routed_tiles(NS // RING, last=True)


def shape_constants():
    c = np.zeros((P, sum(CONST_COLS.values())), np.float32)
    at, p = 0, np.arange(P)
    cols = {
        "ident": np.eye(P), "tri": (p[:, None] < p[None, :]),
        "kmask": ((p[:, None] % 32) // HD == np.arange(2)[None, :]),
        "kv": (p[:, None] // S == np.arange(2)[None, :]),
        "count_down": np.broadcast_to(NE - np.arange(NE), (P, NE)),
        "tile_start": np.broadcast_to(P * np.arange(NT), (P, NT)),
        "slot_tile": np.broadcast_to(np.arange(NS), (P, NS)),
    }
    for name, n in CONST_COLS.items():
        c[:, at:at + n] = cols[name]
        at += n
    ali = np.zeros((2, P + H * S), np.float32)
    ali[0, :P] = 1.0
    ali[1, :P] = p % S
    slopes = np.array([0.5 ** (m * 8 + g * 2 + h) for g in range(4) for m in range(2) for h in range(2)])
    ali[0, P:] = (slopes[:, None] * np.arange(S)[None, :]).reshape(-1)
    ali[1, P:] = np.repeat(-slopes, S)
    return c, ali


_INS = ['x', 'itok_B_0_15', 'itok_B_0_3', 'L0_cond_weight', 'L0_cond_bias', 'L0_attn_Wq', 'L0_attn_bq', 'L0_attn_Aq',
        'L0_attn_Bq', 'L0_attn_Wk', 'L0_attn_bk', 'L0_attn_Ak', 'L0_attn_Bk', 'L0_attn_Wv', 'L0_attn_bv',
        'L0_attn_Av', 'L0_attn_Bv', 'L0_attn_Wo', 'L0_attn_bo', 'L0_attn_Ao', 'L0_attn_Bo', 'L0_attn_rezero',
        'L0_cond2_lora_A', 'L0_cond2_lora_B', 'L0_cond2_lang_embed', 'L0_ffn_Ws1', 'L0_ffn_bs1', 'L0_ffn_Ws2',
        'L0_ffn_bs2', 'L0_ffn_We1', 'L0_ffn_be1', 'L0_ffn_We2', 'L0_ffn_be2', 'L0_ffn_Wr', 'L0_ffn_br']


def kernel(**inputs):
    import concourse.bacc as bacc
    from concourse.bass_utils import run_bass_kernel_spmd

    nc = bacc.Bacc("TRN2", target_bir_lowering=False, num_devices=1)
    consts, alibi = shape_constants()
    given = {name: np.ascontiguousarray(inputs[name]) for name in _INS}
    given["consts"], given["alibi"] = consts, alibi
    arrays, args = {}, {}
    for name, arr in given.items():
        arrays[f"in_{name}_dram"] = arr
        args[name] = nc.dram_tensor(f"in_{name}_dram", arr.shape, mybir.dt.from_np(arr.dtype),
                                    kind="ExternalInput").ap()
    out = nc.dram_tensor("out_0_dram", (TOK + P, D), mybir.dt.float32, kind="ExternalOutput").ap()
    adaln_attn_moe(nc, args, out)
    r = run_bass_kernel_spmd(nc, [arrays], core_ids=[0])
    return r.results[0]["out_0_dram"][:TOK].reshape(B, S, D)
```
